# Optimizing a Trainium2 kernel written in Bass

```python
import numpy as np
import jax
import jax.numpy as jnp

def _softmax(x, axis=-1):
    return jax.nn.softmax(x, axis=axis)

def _gelu(x):
    return jax.nn.gelu(x, approximate=True)

def _silu(x):
    return jax.nn.silu(x)

def _sigmoid(x):
    return jax.nn.sigmoid(x)

def _layernorm(x, axis=-1, eps=1e-05):
    m = jnp.mean(x, axis=axis, keepdims=True)
    v = jnp.var(x, axis=axis, keepdims=True)
    return (x - m) / jnp.sqrt(v + eps)

def _scatter_add(tgt, idx, src, axis=0):
    return tgt.at[idx].add(src)

def _segment_sum(src, seg, n):
    return jax.ops.segment_sum(src, seg, n)
kernel_name = 'mk_flamingo_gated_d1_seqx_r8_f2a926'

def setup_inputs(seed: int=0):
    np.random.seed(seed)
    _w = jnp.asarray

    def _rec_inputs():
        import jax
        import jax.numpy as jnp
        _rk = jax.random.key(seed)
        x = -0.0002928 + 1 * jax.random.normal(jax.random.fold_in(_rk, 1), (8, 256, 128), jnp.float32)
        _lenS = 256 - jax.random.randint(jax.random.fold_in(_rk, 7), (8,), 0, max(1, 256 // 4) + 1, jnp.int32)
        _lenS2 = 512 - jax.random.randint(jax.random.fold_in(_rk, 8), (8,), 0, max(1, 512 // 4) + 1, jnp.int32)
        _ctx_1024P = jax.random.normal(jax.random.fold_in(_rk, 11), (8, 16, 128), jnp.float32)
        _ctx_1024c = jax.random.dirichlet(jax.random.fold_in(_rk, 511), 0.3 * jnp.ones((16,), jnp.float32), (8, 512))
        _ctx_1024t = jnp.einsum('bsk,bkd->bsd', _ctx_1024c, _ctx_1024P)
        _ctx_1024t = _ctx_1024t * jax.lax.rsqrt(jnp.mean(jnp.square(_ctx_1024t)) + 1e-12) * 0.953939
        ctx_1024 = -1.39393e-06 + 0.999914 * (_ctx_1024t + 0.3 * jax.random.normal(jax.random.fold_in(_rk, 611), (8, 512, 128), jnp.float32))
        _validS = jnp.arange(256)[None, :] < _lenS[:, None]
        _validS2 = jnp.arange(512)[None, :] < _lenS2[:, None]
        _causal = jnp.tril(jnp.ones((256, 256), dtype=bool))
        mask_BxSxS2_bf1 = jnp.ones((8, 256, 512), dtype=bool)
        _g = jax.random.normal(jax.random.fold_in(_rk, 9001), (2, 1), jnp.float32)
        _g = jnp.sign(_g) * jnp.maximum(jnp.abs(_g), 1.0) + (_g == 0) * 1.0
        g_xattn = _g[0]
        g_ffn = _g[1]
        return (x, ctx_1024, mask_BxSxS2_bf1, g_xattn, g_ffn)
    x, ctx_1024, mask_BxSxS2_bf1, g_xattn, g_ffn = _rec_inputs()

    def _L0_xattn_setup():
        import jax, jax.numpy as jnp
        import numpy as np
        H = 16
        E = 128
        D = E // H

        def _mha(Q, K, V, mask, Wq, bq, Wk, bk, Wv, bv, Wo, bo):
            B, Nq, _ = Q.shape
            Nk = K.shape[1]
            q = Q @ Wq.T + bq
            k = K @ Wk.T + bk
            v = V @ Wv.T + bv
            q = q.reshape(B, Nq, H, D)
            k = k.reshape(B, Nk, H, D)
            v = v.reshape(B, Nk, H, D)
            scores = jnp.einsum('bqhd,bkhd->bhqk', q, k) / jnp.sqrt(jnp.float32(D))
            scores = jnp.where(mask[:, None, :, :], scores, -jnp.inf)
            attn = jax.nn.softmax(scores, axis=-1)
            x = jnp.einsum('bhqk,bkhd->bqhd', attn, v).reshape(B, Nq, E)
            return x @ Wo.T + bo
        key = jax.random.key(seed)
        ks = jax.random.split(key, 12)
        B, N = (2, 256)
        s = 1.0 / np.sqrt(E).astype(np.float32)
        inp = {'Q': jax.random.normal(ks[0], (B, N, E), jnp.float32), 'K': jax.random.normal(ks[1], (B, N, E), jnp.float32), 'V': jax.random.normal(ks[2], (B, N, E), jnp.float32), 'mask': jnp.ones((B, N, N), dtype=bool), 'Wq': jax.random.normal(ks[3], (E, E), jnp.float32) * s, 'bq': jax.random.normal(ks[4], (E,), jnp.float32) * s, 'Wk': jax.random.normal(ks[5], (E, E), jnp.float32) * s, 'bk': jax.random.normal(ks[6], (E,), jnp.float32) * s, 'Wv': jax.random.normal(ks[7], (E, E), jnp.float32) * s, 'bv': jax.random.normal(ks[8], (E,), jnp.float32) * s, 'Wo': jax.random.normal(ks[9], (E, E), jnp.float32) * s, 'bo': jax.random.normal(ks[10], (E,), jnp.float32) * s}
        return inp
    _L0_xattn_all = _L0_xattn_setup()
    _L0_xattn_in = {k: v for k, v in _L0_xattn_all.items() if k in ('Wq', 'bq', 'Wk', 'bk', 'Wv', 'bv', 'Wo', 'bo')}
    del _L0_xattn_all

    def _L0_ffn_setup():
        import jax, jax.numpy as jnp
        import numpy as np
        E = 16
        K = 4
        B, S, H, I = (4, 128, 128, 256)
        key = jax.random.key(seed)
        k0, k1, k2, k3 = jax.random.split(key, 4)
        scale = 0.02
        return {'hidden_states': jax.random.normal(k0, (B, S, H), jnp.float32), 'router_w': jax.random.normal(k1, (H, E), jnp.float32) * scale, 'router_b': jnp.zeros((E,), jnp.float32), 'w1': jax.random.normal(k2, (E, H, I), jnp.float32) * scale, 'b1': jnp.zeros((E, I), jnp.float32), 'w2': jax.random.normal(k3, (E, I, H), jnp.float32) * scale, 'b2': jnp.zeros((E, H), jnp.float32)}
    _L0_ffn_all = _L0_ffn_setup()
    _L0_ffn_in = {k: v for k, v in _L0_ffn_all.items() if k in ('router_w', 'router_b', 'w1', 'b1', 'w2', 'b2')}
    del _L0_ffn_all
    return {'x': x, 'ctx_1024': ctx_1024, 'mask_BxSxS2_bf1': mask_BxSxS2_bf1, 'g_xattn': g_xattn, 'g_ffn': g_ffn, 'L0_xattn_Wq': _L0_xattn_in['Wq'], 'L0_xattn_bq': _L0_xattn_in['bq'], 'L0_xattn_Wk': _L0_xattn_in['Wk'], 'L0_xattn_bk': _L0_xattn_in['bk'], 'L0_xattn_Wv': _L0_xattn_in['Wv'], 'L0_xattn_bv': _L0_xattn_in['bv'], 'L0_xattn_Wo': _L0_xattn_in['Wo'], 'L0_xattn_bo': _L0_xattn_in['bo'], 'L0_ffn_router_w': _L0_ffn_in['router_w'], 'L0_ffn_router_b': _L0_ffn_in['router_b'], 'L0_ffn_w1': _L0_ffn_in['w1'], 'L0_ffn_b1': _L0_ffn_in['b1'], 'L0_ffn_w2': _L0_ffn_in['w2'], 'L0_ffn_b2': _L0_ffn_in['b2']}

def reference(x, ctx_1024, mask_BxSxS2_bf1, g_xattn, g_ffn, L0_xattn_Wq, L0_xattn_bq, L0_xattn_Wk, L0_xattn_bk, L0_xattn_Wv, L0_xattn_bv, L0_xattn_Wo, L0_xattn_bo, L0_ffn_router_w, L0_ffn_router_b, L0_ffn_w1, L0_ffn_b1, L0_ffn_w2, L0_ffn_b2):
    import jax
    import jax.numpy as jnp

    def _L0_xattn_ref(Q, K, V, mask, Wq, bq, Wk, bk, Wv, bv, Wo, bo):
        import jax, jax.numpy as jnp
        import numpy as np
        H = 16
        E = 128
        D = E // H

        def _mha(Q, K, V, mask, Wq, bq, Wk, bk, Wv, bv, Wo, bo):
            B, Nq, _ = Q.shape
            Nk = K.shape[1]
            q = Q @ Wq.T + bq
            k = K @ Wk.T + bk
            v = V @ Wv.T + bv
            q = q.reshape(B, Nq, H, D)
            k = k.reshape(B, Nk, H, D)
            v = v.reshape(B, Nk, H, D)
            scores = jnp.einsum('bqhd,bkhd->bhqk', q, k) / jnp.sqrt(jnp.float32(D))
            scores = jnp.where(mask[:, None, :, :], scores, -jnp.inf)
            attn = jax.nn.softmax(scores, axis=-1)
            x = jnp.einsum('bhqk,bkhd->bqhd', attn, v).reshape(B, Nq, E)
            return x @ Wo.T + bo
        return _mha(Q, K, V, mask, Wq, bq, Wk, bk, Wv, bv, Wo, bo)

    def _L0_ffn_ref(hidden_states, router_w, router_b, w1, b1, w2, b2):
        import jax, jax.numpy as jnp
        import numpy as np
        E = 16
        K = 4
        B, S, H, I = (4, 128, 128, 256)
        b, s, h = hidden_states.shape
        logits = hidden_states @ router_w + router_b
        probs = jax.nn.softmax(logits, axis=-1)
        topw, topi = jax.lax.top_k(probs, K)
        topw = topw / jnp.sum(topw, axis=-1, keepdims=True)
        combine = jnp.sum(jax.nn.one_hot(topi, E, dtype=hidden_states.dtype) * topw[..., None], axis=2)
        x = hidden_states.reshape(b * s, h)
        c = combine.reshape(b * s, E)

        def body(acc, expert):
            w1e, b1e, w2e, b2e, ce = expert
            hmid = jax.nn.gelu(x @ w1e + b1e, approximate=False)
            return (acc + (hmid @ w2e + b2e) * ce[:, None], None)
        out, _ = jax.lax.scan(body, jnp.zeros_like(x), (w1, b1, w2, b2, c.T))
        return out.reshape(b, s, h)
    x = x + jnp.tanh(g_xattn[0]) * _L0_xattn_ref(_layernorm(x, axis=-1), ctx_1024, ctx_1024, mask_BxSxS2_bf1, L0_xattn_Wq, L0_xattn_bq, L0_xattn_Wk, L0_xattn_bk, L0_xattn_Wv, L0_xattn_bv, L0_xattn_Wo, L0_xattn_bo)
    x = x + jnp.tanh(g_ffn[0]) * _L0_ffn_ref(_layernorm(x, axis=-1), L0_ffn_router_w, L0_ffn_router_b, L0_ffn_w1, L0_ffn_b1, L0_ffn_w2, L0_ffn_b2)
    return x

_drawn_inputs = setup_inputs


def setup_inputs(seed=0):
    import zlib

    import numpy as np

    out = dict(_drawn_inputs(seed))
    spreads = {'L0_ffn_router_b': (0.0, 0.272), 'L0_ffn_b1': (0.0, 0.8), 'L0_ffn_b2': (0.0, 0.1)}
    factors = {'L0_xattn_bq': 3.532, 'L0_xattn_bk': 8.0, 'L0_ffn_w1': 3.451, 'L0_ffn_w2': 3.107}
    for name, (base, spread) in spreads.items():
        noise = np.random.default_rng([zlib.crc32(name.encode()), seed]).standard_normal(out[name].shape)
        drawn = base * np.exp(spread * noise) if base else spread * noise
        out[name] = jnp.asarray(drawn.astype(out[name].dtype))
    for name, factor in factors.items():
        out[name] = (out[name] * factor).astype(out[name].dtype)
    return out
```

```python
from contextlib import ExitStack

import numpy as np

import concourse.bass as bass
from concourse import mybir

F32 = mybir.dt.float32
F32R = mybir.dt.float32r
BF16 = mybir.dt.bfloat16
I32 = mybir.dt.int32
ALU = mybir.AluOpType
ACT = mybir.ActivationFunctionType
AX_X = mybir.AxisListType.X

B, NQ, NK, E = 8, 256, 512, 128
H, D = 16, 8
P = 128
QT, KT = NQ // P, NK // P
G, HG = 4, 4
R = 32
NEXP, TOPK, FF = 16, 4, 256
MT = FF // P
TOK = B * NQ
TT = TOK // P
CH = 512
SC = 3
UNITS_E = MT * 2
AHEAD = 3
SCALE = float(D) ** -0.5
EPS = 1e-5
MASKED = 1e30
LN_STEPS = 2 * QT + 2 + 9
GUESS = float(0x5F3759DF - 2 ** 30 - 2 ** 22)


def stack_selectors():
    sel = np.zeros((P, 4, G, P), np.float32)
    for g in range(G):
        for i in range(HG):
            for d in range(D):
                f, r = (g * HG + i) * D + d, i * R + 2 + d
                for matrix, block in ((0, 0), (0, 1), (1, 2), (2, 0), (3, 1), (2, 2)):
                    sel[f, matrix, g, r + block * D] = 1.0
    ones = np.zeros((P, 1), np.float32)
    for i in range(HG):
        ones[i * R:i * R + 2] = 1.0
    return sel.reshape(P, 4 * G * P), ones


def build(nc, t):
    ctx = ExitStack()
    with ctx:
        def sb(name, shape, dt=F32):
            return ctx.enter_context(nc.sbuf_tensor(name, shape, dt))

        def sem(name):
            return ctx.enter_context(nc.semaphore(name))

        wqkvo = sb("wqkvo", [P, 4, E])
        cols = sb("cols", [P, 4])
        rows = sb("rows", [P, E + NEXP + 2])
        rb_row = rows[:, E:E + NEXP]
        gates = rows[:, E + NEXP:]
        ident = sb("ident", [P, P])
        ident_b = sb("ident_b", [P, P], BF16)
        sel = sb("sel", [P, 4, G, P], F32R)
        notfirst = sb("notfirst", [P, TT * NEXP])
        rw = sb("rw", [P, NEXP])
        b2 = sb("b2", [NEXP, E])
        tgates = sb("tgates", [P, 2])
        tg_bo = sb("tg_bo", [P, E])

        x_sb = sb("x_sb", [P, TT, E])
        ctx_t = sb("ctx_t", [P, 2, NK])
        xn = sb("xn", [P, QT, E])
        xn_t = sb("xn_t", [P, NQ])
        q_hi, q_lo = sb("q_hi", [P, NQ], F32R), sb("q_lo", [P, NQ], F32R)
        k_hi, k_lo = sb("k_hi", [P, NK], F32R), sb("k_lo", [P, NK], F32R)
        k_stack = sb("k_stack", [P, 2, NK])
        k_pad = sb("k_pad", [P, 2, H, NK], F32R)
        q_stack = sb("q_stack", [P, 2, G, NQ], F32R)
        q_shift = sb("q_shift", [P, 2, NQ], F32R)
        v_one = sb("v_one", [P, 2, KT, H, R])
        probs = sb("probs", [P, KT, HG * NQ])
        selraw = probs[:, 0:2, :].rearrange("p t n -> p (t n)")
        maskq_u8 = sb("maskq_u8", [P, QT, NK], mybir.dt.uint8)
        maskt_u8 = sb("maskt_u8", [P, KT, NQ], mybir.dt.uint8)
        maskq = sb("maskq", [P, 2, QT, NK], BF16)
        maskt = sb("maskt", [P, 2, KT, NQ], BF16)
        maxes = sb("maxes", [P, 2, QT, H])
        neg_m = sb("neg_m", [P, 2, QT, P])
        out_g = sb("out_g", [P, G, NQ])
        dead = sb("dead", [P, QT, H])
        inv = sb("inv", [P, 2, H])
        attn = sb("attn", [P, QT, E])
        attn_t = sb("attn_t", [P, NQ])
        x_bo = sb("x_bo", [P, QT, E])
        x1 = sb("x1", [P, QT, E])
        xn2 = sb("xn2", [P, QT, E])
        xn2_t = sb("xn2_t", [P, NQ])
        stats = sb("stats", [P, 2, TT, 6])
        meanvar = sb("meanvar", [P, 2, TT, 2])
        rstd = sb("rstd", [P, 2, 3, TT])
        x1_t = sb("x1_t", [P, TOK])
        h_hi, h_lo = sb("h_hi", [P, TOK], F32R), sb("h_lo", [P, TOK], F32R)
        logits = sb("logits", [P, TT, NEXP])
        top8 = sb("top8", [P, TT, 8])
        rt = sb("rt", [P, 4, TT, NEXP])
        rs = sb("rs", [P, 4, TT])
        cw_t = x_sb[0:NEXP, :, :].rearrange("p t f -> p (t f)")

        banks = ctx.enter_context(nc.psum_tensor("banks", [P, 8, CH], F32))
        sc = [banks[:, n, :] for n in range(SC)]
        st = [banks[:, 3, :], banks[:, 4, :]]
        ov = banks[:, 5, 0:NQ]
        misc = [banks[:, 6, :], banks[:, 7, :]]
        hid = [banks[:, 0:2, :], banks[:, 2:4, :]]
        acc = [banks[:, 4 + c, :] for c in range(4)]

        MISC = [("heads_t0", -1), ("heads_t1", -1), ("max_t1", 0), ("xn_t", 1), ("attn_t", -1), ("q", 1), ("k", 1),
                ("v", 1), ("q_stack0", 1), ("q_stack1", 1), ("max_t2", 0), ("wo", -1), ("k_stack0", 1),
                ("k_stack1", 1), ("k_stack2", 1), ("k_stack3", 1), ("max_t3", 0), ("x1_t", -1), ("logits", -1),
                ("max_t0", 1)]
        MISC_AT = {task: n for n, (task, _) in enumerate(MISC)}

        def bank_of(task):
            return MISC_AT[task] % 2

        ld_x0, ld_x, ld_w, ld_ident, ld_c, ld_sel = (sem(n) for n in ("ld_x0", "ld_x", "ld_w", "ld_ident", "ld_c", "ld_sel"))
        ld_ctx = [sem("ld_ctx0"), sem("ld_ctx1")]
        ld_mask = sem("ld_mask")
        ld_exp = [sem("ld_exp0"), sem("ld_exp1")]
        st_cw, st_out = sem("st_cw"), sem("st_out")
        ld_cw = [sem("ld_cw0"), sem("ld_cw1")]
        ident_ok, zeroed, zeroed_v, sel_ok, tanh_ok, bvo_full, bvo_ok, tgbo_ok = (sem(n) for n in (
            "ident_ok", "zeroed", "zeroed_v", "sel_ok", "tanh_ok", "bvo_full", "bvo_ok", "tgbo_ok"))
        xnt_full, q_full, k_full, v_full, qs_full, ks_full, mt_full, ht_full, at_full, wo_full, x1t_full, lg_full = (
            sem(n + "_full") for n in ("xnt", "q", "k", "v", "qs", "ks", "mt", "ht", "at", "wo", "x1t", "lg"))
        sc_full, max_done, st_full, exp_done, pv_done, heads_out = (sem(n) for n in (
            "sc_full", "max_done", "st_full", "exp_done", "pv_done", "heads_out"))
        ln_done = [sem("ln1_done"), sem("ln2_done")]
        ln_step = [sem("ln1_step"), sem("ln2_step")]
        xnt_ok, qhi_ok, qlo_ok, khi_ok, klo_ok, v_ok, qs_ok, ks_ok, pad_ok, mask_ok = (sem(n) for n in (
            "xnt_ok", "qhi_ok", "qlo_ok", "khi_ok", "klo_ok", "v_ok", "qs_ok", "ks_ok", "pad_ok", "mask_ok"))
        negm_hi, negm_ok, qshift_ok, norm_step, attn_ok, attnt_ok, xbo_ok, x1_ok, xn2t_ok, x1t_ok, hhi_ok, hlo_ok, lg_ok = (
            sem(n) for n in ("negm_hi", "negm_ok", "qshift_ok", "norm_step", "attn_ok", "attnt_ok", "xbo_ok",
                             "x1_ok", "xn2t_ok", "x1t_ok", "hhi_ok", "hlo_ok", "lg_ok"))
        rt_step, z_ok, rexp_ok, cw_ok, cwt_full, cwt_ok = (sem(n) for n in (
            "rt_step", "z_ok", "rexp_ok", "cw_ok", "cwt_full", "cwt_ok"))
        w_hi_ok, w_lo_ok, hid_full, gelu_ok, gw_ok, g_hi_ok, g_lo_ok, ff_done, out_ok = (sem(n) for n in (
            "w_hi_ok", "w_lo_ok", "hid_full", "gelu_ok", "gw_ok", "g_hi_ok", "g_lo_ok", "ff_done", "out_ok"))

        WCOLS = FF + MT * E
        HALF = 2 * CH
        w_raw = sb("w_raw", [P, 2, WCOLS + MT])
        under = k_pad[:, 0, :, :].rearrange("p h n -> p (h n)")
        w_hi = [under[:, n * WCOLS:(n + 1) * WCOLS] for n in (0, 1)]
        w_lo = [under[:, n * WCOLS:(n + 1) * WCOLS] for n in (2, 3)]
        g_hi = [under[:, n * HALF:(n + 1) * HALF] for n in (2, 3)]
        g_lo = [under[:, n * HALF:(n + 1) * HALF] for n in (4, 5)]
        gel = [probs[:, n, :] for n in (0, 1)]
        gw = [probs[:, n, :] for n in (2, 3)]
        under = v_one[:, :, :, :, :].rearrange("p a t h r -> p (a t h r)")
        cw = [under[:, n * TOK:(n + 1) * TOK] for n in (0, 1)]

        block = ctx.enter_context(nc.Block())

        def wait(eng, s, n):
            if not (isinstance(n, int) and n <= 0):
                eng.wait_ge(s, n)

        def wait_apart(eng, s, n):
            n = n if isinstance(n, int) else eng.to_reg(n)
            eng.wait_ge(ld_x0, 16)
            eng.wait_ge(s, n)

        def ctx_count(b, p):
            return b * 8 + (16 if p == 0 else 8)

        @block.sync
        def _(sp):
            sp.dma_start(x_sb[:, 0:QT, :], t["x"][0:NQ, :].rearrange("(t p) f -> p t f", p=P)).then_inc(ld_x0, 16)
            sp.dma_start(ident[:, :], t["ident"]).then_inc(ld_ident, 16)
            sp.dma_start(wqkvo[:, :, :], t["wqkvo"].rearrange("p (m f) -> p m f", m=4)).then_inc(ld_w, 16)
            sp.dma_start(ctx_t[:, 0, :], t["ctx_t"][0]).then_inc(ld_ctx[0], 16)
            sp.dma_start(cols[:, :], t["cols"]).then_inc(ld_w, 16)
            sp.dma_start(rows[:, :], t["rows"].partition_broadcast(P)).then_inc(ld_w, 16)
            sp.dma_start(maskq_u8[:, :, :], t["maskq"][0].rearrange("(t p) k -> p t k", p=P)).then_inc(ld_mask, 16)
            sp.dma_start(maskt_u8[:, :, :], t["maskt"][0].rearrange("(t p) q -> p t q", p=P)).then_inc(ld_mask, 16)
            sp.dma_start(selraw, t["sel"]).then_inc(ld_sel, 16)
            sp.dma_start(x_sb[:, QT:, :], t["x"][NQ:, :].rearrange("(t p) f -> p t f", p=P)).then_inc(ld_x, 16)
            sp.dma_start(ctx_t[:, 1, :], t["ctx_t"][1]).then_inc(ld_ctx[1], 16)
            sp.dma_start(notfirst[:, :], t["notfirst"].partition_broadcast(P)).then_inc(ld_c, 16)
            sp.dma_start(rw[:, :], t["router_w"]).then_inc(ld_c, 16)
            sp.dma_start(b2[:, :], t["b2"]).then_inc(ld_c, 16)
            for e in range(2):
                sp.dma_start(w_raw[:, e, :], t["experts"][e]).then_inc(ld_exp[e], 16)

            def masks(b):
                wait_apart(sp, mask_ok, b * 2)
                sp.dma_start(maskq_u8[:, :, :], t["maskq"][b].rearrange("(t p) k -> p t k", p=P)).then_inc(ld_mask, 16)
                sp.dma_start(maskt_u8[:, :, :], t["maskt"][b].rearrange("(t p) q -> p t q", p=P)).then_inc(ld_mask, 16)

            masks(1)
            with sp.Fori(0, B - 3, 2) as i:
                for p in range(2):
                    b = i + p
                    wait_apart(sp, v_full, b + 1)
                    sp.dma_start(ctx_t[:, p, :], t["ctx_t"][b + 2]).then_inc(ld_ctx[p], 16)
                    masks(b + 2)
            sp.wait_ge(cwt_ok, 4)
            sp.dma_start(t["cw"], cw_t[:, :]).then_inc(st_cw, 16)
            sp.wait_ge(st_cw, 16)
            for e in range(2):
                sp.dma_start(cw[e], t["cw"][e:e + 1, :].partition_broadcast(P)).then_inc(ld_cw[e], 16)

            def next_expert(e, p):
                wait_apart(sp, ff_done, e * UNITS_E + 2)
                wait_apart(sp, gelu_ok, e * UNITS_E + UNITS_E)
                sp.dma_start(w_raw[:, p, :], t["experts"][e + 2]).then_inc(ld_exp[p], 16)
                wait_apart(sp, gw_ok, e * UNITS_E + UNITS_E)
                sp.dma_start(cw[p], t["cw"][bass.ds(e + 2, 1), :].partition_broadcast(P)).then_inc(ld_cw[p], 16)

            with sp.Fori(0, NEXP - 3, 2) as i:
                for p in range(2):
                    next_expert(i + p, p)
            for c in range(4):
                sp.wait_ge(out_ok, c + 1)
                sp.dma_start(t["out"][:, c * CH:(c + 1) * CH], x1_t[:, c * CH:(c + 1) * CH]).then_inc(st_out, 16)
            sp.wait_ge(st_out, 4 * 16)

        @block.gpsimd
        def _(pool):
            def zero_pad(p):
                for g in range(G):
                    pool.memset(k_pad[:, p, HG * g:HG * (g + 1), :].bitcast(F32), 0.0).then_inc(zeroed, 1)

            def mask_bias(b, p):
                pool.wait_ge(ld_mask, b * 32 + 32)
                if not isinstance(b, int) or b >= 2:
                    wait_apart(pool, exp_done, b * 32 - 32)
                    pool.wait_ge(max_done, b * 32 - 32)
                pool.tensor_scalar(maskq[:, p, :, :], maskq_u8[:, :, :], -1.0, MASKED, ALU.add, ALU.mult).then_inc(mask_ok, 1)
                pool.tensor_scalar(maskt[:, p, :, :], maskt_u8[:, :, :], -1.0, MASKED, ALU.add, ALU.mult).then_inc(mask_ok, 1)

            def x_plus_bo(b):
                if isinstance(b, int) and b == 0:
                    pool.wait_ge(tgbo_ok, 1)
                bo = tg_bo[:, :].unsqueeze(1).to_broadcast([P, QT, E])
                pool.tensor_tensor(x_bo[:, :, :], x_sb[:, bass.ds(b * QT, QT), :], bo, ALU.add).then_inc(xbo_ok, 1)

            def h_halves(b):
                wait_apart(pool, xn2t_ok, b + 1)
                cols_b = bass.ds(b * NQ, NQ)
                pool.tensor_copy(h_hi[:, cols_b], xn2_t[:, :]).then_inc(hhi_ok, 1)
                wait_apart(pool, hhi_ok, b + 1)
                pool.tensor_tensor(h_lo[:, cols_b], xn2_t[:, :], h_hi[:, cols_b].bitcast(F32), ALU.subtract).then_inc(hlo_ok, 1)

            def pad(b, p, g):
                if g == 0:
                    pool.wait_ge(mask_ok, b * 2 + 2)
                wait_apart(pool, ks_ok, b * G + g + 1)
                if isinstance(b, int) and b < 2:
                    pool.wait_ge(zeroed, b * G + g + 1)
                for i in range(HG):
                    last = pool.tensor_scalar(k_pad[R * i:R * (i + 1), p, HG * g + i, :], k_stack[R * i:R * (i + 1), g % 2, :],
                                              1.0, 0.0, ALU.mult, ALU.add)
                last.then_inc(pad_ok, 1)

            def batch(b, p):
                mask_bias(b, p)
                for g in range(G):
                    pad(b, p, g)
                wait_apart(pool, pad_ok, b * G + G)
                if not isinstance(b, int) or b >= 2:
                    h_halves(b - 2)
                x_plus_bo(b - 1)

            zero_pad(0)
            mask_bias(0, 0)
            for g in range(G):
                pad(0, 0, g)
            pool.wait_ge(pad_ok, G)
            zero_pad(1)
            pool.wait_ge(ld_x, 16)
            batch(1, 1)
            with pool.Fori(2, B - 1, 2) as i:
                batch(i, 0)
                batch(i + 1, 1)
            h_halves(B - 2)
            x_plus_bo(B - 1)
            h_halves(B - 1)

            def weight_halves(e, p):
                pool.wait_ge(ld_exp[p], e * 8 + (16 if p == 0 else 8))
                if isinstance(e, int) and e < 2:
                    pool.wait_ge(exp_done, B * 32)
                else:
                    wait_apart(pool, ff_done, e * UNITS_E - UNITS_E)
                pool.tensor_scalar(w_hi[p], w_raw[:, p, 0:WCOLS], 1.0, 0.0, ALU.mult, ALU.add).then_inc(w_hi_ok, 1)
                pool.wait_ge(w_hi_ok, e + 1)
                pool.tensor_tensor(w_lo[p], w_raw[:, p, 0:WCOLS], w_hi[p].bitcast(F32), ALU.subtract).then_inc(w_lo_ok, 1)

            weight_halves(0, 0)
            weight_halves(1, 1)
            with pool.Fori(2, NEXP - 1, 2) as i:
                weight_halves(i, 0)
                weight_halves(i + 1, 1)

        @block.scalar
        def _(act):
            act.wait_ge(ld_w, 48)
            act.activation(tgates[:, :], gates, ACT.Tanh).then_inc(tanh_ok, 1)

            def xn_t_copy(b):
                act.wait_ge(xnt_full, b + 1)
                act.activation(xn_t[:, :], misc[bank_of("xn_t")][:, 0:NQ], ACT.Copy).then_inc(xnt_ok, 1)

            def q_hi_half(b):
                act.wait_ge(q_full, b + 1)
                wait(act, qs_full, b * 2)
                act.activation(q_hi[:, :], misc[bank_of("q")][:, 0:NQ], ACT.Identity, bias=cols[:, 0:1]).then_inc(qhi_ok, 1)

            def k_hi_half(b):
                act.wait_ge(k_full, b + 1)
                wait(act, ks_full, b * G)
                act.activation(k_hi[:, :], misc[bank_of("k")], ACT.Identity, bias=cols[:, 1:2]).then_inc(khi_ok, 1)

            def q_stack_out(b, p, n):
                act.wait_ge(qs_full, b * 2 + n + 1)
                bank = bank_of(f"q_stack{n}")
                act.activation(q_stack[:, p, 2 * n:2 * n + 2, :].rearrange("p g q -> p (g q)"), misc[bank],
                               ACT.Copy).then_inc(qs_ok, 1)

            def k_stack_out(b, g):
                act.wait_ge(ks_full, b * G + g + 1)
                if not (isinstance(b, int) and b == 0 and g < 2):
                    act.wait_ge(pad_ok, b * G + g - 1)
                bank = bank_of(f"k_stack{g}")
                act.activation(k_stack[:, g % 2, :], misc[bank], ACT.Identity, bias=cols[:, 2:3]).then_inc(ks_ok, 1)

            def v_out(b, p):
                act.wait_ge(v_full, b + 1)
                if not isinstance(b, int) or b >= 2:
                    act.wait_ge(pv_done, b * 16 - 16)
                act.activation(v_one[:, p, :, :, 0:D].rearrange("p t h d -> p (t h) d"),
                               misc[bank_of("v")].rearrange("p (h d) -> p h d", d=D), ACT.Copy).then_inc(v_ok, 1)

            def exp(b, g, j):
                kt, pair = j // 2, j % 2
                act.wait_ge(st_full, b * 32 + g * 8 + j + 1)
                if pair == 0:
                    wait(act, pv_done, b * 16 + g * 4 - 3 + kt)
                act.activation(probs[:, kt, pair * CH:(pair + 1) * CH], st[j % 2], ACT.Exp, scale=SCALE).then_inc(exp_done, 1)

            def heads_copy(b, g):
                act.wait_ge(pv_done, b * 16 + g * 4 + 4)
                act.activation(out_g[:, g, :], ov, ACT.Copy).then_inc(heads_out, 1)

            def attn_t_copy(b):
                act.wait_ge(at_full, b + 1)
                bank = bank_of("attn_t")
                act.activation(attn_t[:, :], misc[bank][:, 0:NQ], ACT.Copy).then_inc(attnt_ok, 1)

            def x1_t_copy(b):
                act.wait_ge(x1t_full, b + 1)
                bank = bank_of("x1_t")
                act.activation(xn2_t[:, :], misc[bank][:, 0:NQ], ACT.Copy).then_inc(xn2t_ok, 1)
                act.activation(x1_t[:, bass.ds(b * NQ, NQ)], misc[bank][:, NQ:], ACT.Copy).then_inc(x1t_ok, 1)

            def slots(b, p, before=None, after=None):
                for g in range(G):
                    for j in range(8):
                        exp(b, g, j)
                        if j == 2 and (before or g):
                            if g:
                                heads_copy(b, g - 1)
                            else:
                                heads_copy(b - 1, G - 1)
                        if g == 1:
                            if j == 0 and after:
                                xn_t_copy(b + 1)
                            if j == 1 and before:
                                attn_t_copy(b - 1)
                            if j == 2 and after:
                                q_hi_half(b + 1)
                            if j == 3 and after:
                                k_hi_half(b + 1)
                            if j == 4 and after:
                                v_out(b + 1, 1 - p)
                            if j in (5, 6) and after:
                                q_stack_out(b + 1, 1 - p, j - 5)
                        if g == 2 and 1 <= j <= 4 and after:
                            k_stack_out(b + 1, j - 1)
                        if g == 3 and j == 1 and before:
                            x1_t_copy(b - 1)

            xn_t_copy(0)
            q_hi_half(0)
            k_hi_half(0)
            act.wait_ge(zeroed_v, 4)
            v_out(0, 0)
            q_stack_out(0, 0, 0)
            q_stack_out(0, 0, 1)
            for g in range(G):
                k_stack_out(0, g)
            slots(0, 0, before=False, after=True)
            with act.Fori(1, B - 2, 2) as i:
                slots(i, 1, before=True, after=True)
                slots(i + 1, 0, before=True, after=True)
            slots(B - 1, 1, before=True, after=False)
            heads_copy(B - 1, G - 1)
            attn_t_copy(B - 1)
            x1_t_copy(B - 1)

            act.wait_ge(z_ok, 1)
            act.activation(rt[:, 1, :, :], rt[:, 0, :, :], ACT.Exp).then_inc(rexp_ok, 1)

            def gelu(e, k, p):
                v = e * UNITS_E + k
                act.wait_ge(hid_full, v + 1)
                wait(act, gw_ok, v - 1)
                mt = k // 2
                act.activation(gel[k % 2], hid[k % 2].rearrange("p a c -> p (a c)"), ACT.Gelu,
                               bias=w_raw[:, p, WCOLS + mt:WCOLS + mt + 1]).then_inc(gelu_ok, 1)

            def hi_half(v, par):
                act.wait_ge(gw_ok, v + 1)
                wait(act, ff_done, v - 1)
                act.activation(g_hi[par], gw[par], ACT.Copy).then_inc(g_hi_ok, 1)

            def expert(e, p, first=False):
                for k in range(UNITS_E):
                    gelu(e, k, p)
                    if not (first and k == 0):
                        hi_half(e * UNITS_E + k - 1, (k - 1) % 2)

            expert(0, 0, first=True)
            expert(1, 1)
            with act.Fori(2, NEXP - 1, 2) as i:
                expert(i, 0)
                expert(i + 1, 1)
            hi_half(NEXP * UNITS_E - 1, 1)

        @block.vector
        def _(dve):
            def statistics(n, base, src, at, part):
                count = [(0, 2 * len(src), 2 * len(src) + 5)[part]]

                def step(ins):
                    count[0] += 1
                    ins.then_inc(ln_step[n], 1)
                    dve.wait_ge(ln_step[n], base + count[0])

                half, y, tmp = (rstd[:, n, k, at] for k in range(3))
                if part == 0:
                    for q, tile in enumerate(src):
                        dve.bn_stats(stats[:, n, at.start + q, :], tile).then_inc(ln_step[n], 1)
                    count[0] += len(src)
                    wait_apart(dve, ln_step[n], base + count[0])
                    for q in range(len(src)):
                        dve.bn_aggr(meanvar[:, n, at.start + q, :], stats[:, n, at.start + q, :]).then_inc(ln_step[n], 1)
                    count[0] += len(src)
                    dve.wait_ge(ln_step[n], base + count[0])
                if part == 1:
                    step(dve.tensor_scalar(half, meanvar[:, n, at, 1], EPS, -0.5, ALU.add, ALU.mult))
                    step(dve.tensor_scalar(y.bitcast(I32), half.bitcast(I32), -0.5, GUESS, ALU.mult, ALU.add))
                if part in (1, 2):
                    for _ in range(part):
                        step(dve.tensor_tensor(tmp, y, y, ALU.mult))
                        step(dve.tensor_tensor(tmp, tmp, half, ALU.mult))
                        step(dve.scalar_tensor_tensor(out=y, in0=tmp, scalar=1.5, in1=y, op0=ALU.add, op1=ALU.mult))

            def ln_x_statistics(lo, hi, part):
                base = 0 if lo == 0 else LN_STEPS
                statistics(0, base, [x_sb[:, n, :] for n in range(lo, hi)], slice(lo, hi), part)

            def ln_x(b):
                wait(dve, xnt_full, b)
                for q in range(QT):
                    n = b * QT + q
                    if isinstance(n, int):
                        n = slice(n, n + 1)
                    else:
                        n = bass.ds(n, 1)
                    dve.tensor_scalar(xn[:, q, :], x_sb[:, n, :].rearrange("p t f -> p (t f)"), meanvar[:, 0, n, 0],
                                      rstd[:, 0, 1, n], ALU.subtract, ALU.mult).then_inc(ln_done[0], 1)

            def ln_x1(b, part):
                if part == 0:
                    dve.wait_ge(x1_ok, b + 1)
                if part < 3:
                    statistics(1, b * LN_STEPS, [x1[:, q, :] for q in range(QT)], slice(0, QT), part)
                else:
                    for q in range(QT):
                        dve.tensor_scalar(xn2[:, q, :], x1[:, q, :], meanvar[:, 1, q, 0:1], rstd[:, 1, 1, q:q + 1],
                                          ALU.subtract, ALU.mult).then_inc(ln_done[1], 1)

            def q_lo_half(b):
                dve.wait_ge(qhi_ok, b + 1)
                dve.scalar_tensor_tensor(out=q_lo[:, :], in0=misc[bank_of("q")][:, 0:NQ], scalar=cols[:, 0:1],
                                         in1=q_hi[:, :].bitcast(F32), op0=ALU.add, op1=ALU.subtract).then_inc(qlo_ok, 1)

            def k_lo_half(b):
                dve.wait_ge(khi_ok, b + 1)
                dve.scalar_tensor_tensor(out=k_lo[:, :], in0=misc[bank_of("k")], scalar=cols[:, 1:2],
                                         in1=k_hi[:, :].bitcast(F32), op0=ALU.add, op1=ALU.subtract).then_inc(klo_ok, 1)

            def row_max(b, p, g, k):
                qt, i = k // HG, k % HG
                if g == 0 and k == 0:
                    dve.wait_ge(mask_ok, b * 2 + 1)
                wait_apart(dve, sc_full, b * 32 + (g * 8 + k + 1))
                h = HG * g + i
                dve.tensor_tensor_reduce(sc[k % SC], sc[k % SC], maskq[:, p, qt, :], 1.0, -3.0e38, ALU.add, ALU.max,
                                         maxes[:, p, qt, h:h + 1]).then_inc(max_done, 1)

            def minus_max(b, p, g):
                dve.wait_ge(max_done, b * 32 + (g * 8 + 8))
                if not (isinstance(b, int) and b == 0 and g < 2):
                    dve.wait_ge(mt_full, b * 4 + (g - 1))
                m = maxes[:, p, :, HG * g:HG * (g + 1)]
                col = neg_m[:, g % 2, :, :].rearrange("p q (i r) -> p q i r", r=R)
                dve.tensor_scalar(col[:, :, :, 0].bitcast(F32R), m, -1.0, None, ALU.mult).then_inc(negm_hi, 1)
                dve.wait_ge(negm_hi, b * 4 + (g + 1))
                dve.scalar_tensor_tensor(out=col[:, :, :, 1], in0=m, scalar=-1.0, in1=col[:, :, :, 0], op0=ALU.mult,
                                         op1=ALU.subtract).then_inc(negm_ok, 1)

            def shift(b, p, g):
                dve.wait_ge(mt_full, b * 4 + (g + 1))
                if g % 2 == 0:
                    dve.wait_ge(qs_ok, b * 2 + (g // 2 + 1))
                if not (isinstance(b, int) and b == 0 and g < 2):
                    dve.wait_ge(st_full, b * 32 + (g * 8 - 8))
                dve.tensor_tensor(q_shift[:, g % 2, :], misc[bank_of(f"max_t{g}")][:, 0:NQ], q_stack[:, p, g, :].bitcast(F32),
                                  ALU.add).then_inc(qshift_ok, 1)

            def normalise(b, p, q):
                heads = misc[bank_of(f"heads_t{q}")].rearrange("p (h r) -> p h r", r=R)
                dve.wait_ge(ht_full, b * 2 + (q + 1))
                dve.reciprocal(inv[:, 0, :], heads[:, :, D]).then_inc(norm_step, 1)
                dve.tensor_scalar(dead[:, 0, :], maxes[:, p, q, :], -1.0, -MASKED / 2, ALU.mult, ALU.add).then_inc(norm_step, 1)
                dve.wait_ge(norm_step, b * 8 + (q * 4 + 2))
                dve.tensor_scalar(dead[:, 1, :], dead[:, 0, :], 0.0, MASKED, ALU.max, ALU.mult).then_inc(norm_step, 1)
                dve.wait_ge(norm_step, b * 8 + (q * 4 + 3))
                dve.scalar_tensor_tensor(out=inv[:, 1, :], in0=dead[:, 1, :], scalar=0.0, in1=inv[:, 0, :], op0=ALU.mult,
                                         op1=ALU.add).then_inc(norm_step, 1)
                dve.wait_ge(norm_step, b * 8 + (q * 4 + 4))
                dve.tensor_tensor(attn[:, q, :].rearrange("p (h d) -> p h d", d=D), heads[:, :, 0:D],
                                  inv[:, 1, :].unsqueeze(2).to_broadcast([P, H, D]), ALU.mult).then_inc(attn_ok, 1)

            def residual(b, p):
                dve.wait_ge(wo_full, b + 1)
                dve.wait_ge(xbo_ok, b + 1)
                dve.scalar_tensor_tensor(out=x1[:, :, :].rearrange("p t f -> p (t f)"), in0=misc[bank_of("wo")][:, 0:QT * E],
                                         scalar=tgates[:, 0:1], in1=x_bo[:, :, :].rearrange("p t f -> p (t f)"),
                                         op0=ALU.mult, op1=ALU.add).then_inc(x1_ok, 1)

            def logits_out(b):
                dve.wait_ge(lg_full, b + 1)
                dve.tensor_tensor(logits[:, bass.ds(b * QT, QT), :],
                                  misc[bank_of("logits")][:, 0:QT * NEXP].rearrange("p (t e) -> p t e", e=NEXP),
                                  rb_row.unsqueeze(1).to_broadcast([P, QT, NEXP]), ALU.add).then_inc(lg_ok, 1)

            def slots(b, p, before=None, after=None):
                for g in range(G):
                    last = g == G - 1 and not after
                    for k in range(8):
                        if not last:
                            if g < G - 1:
                                row_max(b, p, g + 1, k)
                            else:
                                row_max(b + 1, 1 - p, 0, k)
                        if k == 7 and not last:
                            if g < G - 1:
                                minus_max(b, p, g + 1)
                            else:
                                minus_max(b + 1, 1 - p, 0)
                        if g == 0:
                            if not before and k < 3:
                                if k == 0:
                                    dve.wait_ge(ld_x, 16)
                                ln_x_statistics(QT, TT, k)
                            if k == 3 and after:
                                ln_x(b + 1)
                            if k == 5 and before:
                                normalise(b - 1, 1 - p, 0)
                            if k == 7 and before:
                                normalise(b - 1, 1 - p, 1)
                        if g == 1 and after:
                            if k == 3:
                                q_lo_half(b + 1)
                            if k == 5:
                                k_lo_half(b + 1)
                        if g == 2 and before:
                            if k == 0:
                                residual(b - 1, 1 - p)
                            if k in (1, 2, 3, 4):
                                ln_x1(b - 1, k - 1)
                        if g == 3 and before:
                            if k == 5:
                                logits_out(b - 1)
                    if not last:
                        if g < G - 1:
                            shift(b, p, g + 1)
                        else:
                            shift(b + 1, 1 - p, 0)

            dve.wait_ge(ld_x0, 16)
            for part in range(3):
                ln_x_statistics(0, QT, part)
            ln_x(0)
            dve.memset(neg_m[:, :, :, :], 0.0).then_inc(zeroed_v, 1)
            dve.wait_ge(ld_ident, 16)
            dve.tensor_copy(ident_b[:, :], ident[:, :]).then_inc(ident_ok, 1)
            dve.wait_ge(ld_w, 48)
            dve.tensor_copy(attn[:, 0, :], cols[:, 3:4].to_broadcast([P, P])).then_inc(bvo_ok, 1)
            q_lo_half(0)
            k_lo_half(0)
            dve.wait_ge(ld_sel, 16)
            dve.tensor_copy(sel[:, :, :, :].rearrange("p m g r -> p (m g r)"), selraw).then_inc(sel_ok, 1)
            for p in range(2):
                dve.memset(v_one[:, p, :, :, :], 0.0).then_inc(zeroed_v, 1)
            dve.wait_ge(zeroed_v, 3)
            dve.memset(v_one[:, :, :, :, D:D + 1].rearrange("p a t h r -> p (a t h) r"), 1.0).then_inc(zeroed_v, 1)
            dve.wait_ge(bvo_full, 1)
            dve.tensor_tensor(tg_bo[:, :], banks[:, 5, 0:E], rows[:, 0:E], ALU.add).then_inc(bvo_ok, 1)
            dve.wait_ge(bvo_ok, 2)
            dve.wait_ge(tanh_ok, 1)
            dve.tensor_scalar(tg_bo[:, :], tg_bo[:, :], tgates[:, 0:1], None, ALU.mult).then_inc(tgbo_ok, 1)
            for k in range(8):
                row_max(0, 0, 0, k)
            minus_max(0, 0, 0)
            shift(0, 0, 0)
            slots(0, 0, before=False, after=True)
            with dve.Fori(1, B - 2, 2) as i:
                slots(i, 1, before=True, after=True)
                slots(i + 1, 0, before=True, after=True)
            slots(B - 1, 1, before=True, after=False)
            normalise(B - 1, 1, 0)
            normalise(B - 1, 1, 1)
            residual(B - 1, 1)
            for part in range(4):
                ln_x1(B - 1, part)
            logits_out(B - 1)

            count = [0]

            def step(ins):
                count[0] += 1
                ins.then_inc(rt_step, 1)
                dve.wait_ge(rt_step, count[0])

            def bc(a):
                return a.unsqueeze(2).to_broadcast([P, TT, NEXP])

            z, ez, pr, tmp = (rt[:, k, :, :] for k in range(4))
            low, total, above, _ = (rs[:, k, :] for k in range(4))
            dve.wait_ge(lg_ok, B)
            step(dve.tensor_reduce(low, logits[:, :, :], AX_X, ALU.max))
            dve.tensor_tensor(z, logits[:, :, :], bc(low), ALU.subtract).then_inc(z_ok, 1)
            dve.wait_ge(rexp_ok, 1)
            step(dve.tensor_reduce(total, ez, AX_X, ALU.add))
            step(dve.reciprocal(total, total))
            step(dve.tensor_tensor(pr, ez, bc(total), ALU.mult))
            for n in range(TT):
                step(dve.max(top8[:, n, :], rt[:, 2, n, :])) if n == TT - 1 else dve.max(top8[:, n, :], rt[:, 2, n, :])
            fourth = bc(top8[:, :, TOPK - 1])
            step(dve.tensor_tensor(z, pr, fourth, ALU.is_gt))
            step(dve.tensor_reduce(above, z, AX_X, ALU.add))
            step(dve.tensor_tensor(ez, pr, fourth, ALU.is_equal))
            flat = [rt[:, k, :, :].rearrange("p t e -> p (t e)") for k in range(4)]
            dve.wait_ge(ld_c, 48)
            step(dve.tensor_tensor_scan(flat[3], notfirst[:, :], flat[1], 0.0, ALU.mult, ALU.add))
            step(dve.tensor_tensor(tmp, tmp, bc(above), ALU.add))
            step(dve.scalar_tensor_tensor(out=flat[3], in0=flat[3], scalar=float(TOPK), in1=flat[1], op0=ALU.is_le, op1=ALU.mult))
            step(dve.tensor_tensor(z, z, tmp, ALU.add))
            step(dve.tensor_tensor(z, z, pr, ALU.mult))
            step(dve.tensor_reduce(total, z, AX_X, ALU.add))
            step(dve.reciprocal(total, total))
            dve.tensor_tensor(ez, z, bc(total), ALU.mult).then_inc(cw_ok, 1)
            for c in range(4):
                dve.wait_ge(cwt_full, c + 1)
                dve.tensor_copy(cw_t[:, c * CH:(c + 1) * CH], acc[c][0:NEXP, :]).then_inc(cwt_ok, 1)

            def weigh(e, k, p):
                v = e * UNITS_E + k
                half = k % 2
                dve.wait_ge(gelu_ok, v + 1)
                if k == 0:
                    dve.wait_ge(ld_cw[p], e * 8 + (16 if p == 0 else 8))
                if not (isinstance(e, int) and e == 0 and k < 2):
                    dve.wait_ge(g_hi_ok, v - 1)
                    dve.wait_ge(g_lo_ok, v - 1)
                dve.tensor_tensor(gw[k % 2], gel[k % 2], cw[p][:, half * HALF:(half + 1) * HALF], ALU.mult).then_inc(gw_ok, 1)

            def lo_half(v, par):
                dve.wait_ge(g_hi_ok, v + 1)
                dve.tensor_tensor(g_lo[par], gw[par], g_hi[par].bitcast(F32), ALU.subtract).then_inc(g_lo_ok, 1)

            def expert(e, p, first=False):
                for k in range(UNITS_E):
                    weigh(e, k, p)
                    if not (first and k == 0):
                        lo_half(e * UNITS_E + (k - 1), (k - 1) % 2)

            expert(0, 0, first=True)
            expert(1, 1)
            with dve.Fori(2, NEXP - 1, 2) as i:
                expert(i, 0)
                expert(i + 1, 1)
            lo_half(NEXP * UNITS_E - 1, 1)
            dve.wait_ge(ff_done, NEXP * UNITS_E)
            for c in range(4):
                cols_c = x1_t[:, c * CH:(c + 1) * CH]
                dve.scalar_tensor_tensor(out=cols_c, in0=acc[c], scalar=tgates[:, 1:2], in1=cols_c, op0=ALU.mult,
                                         op1=ALU.add).then_inc(out_ok, 1)

        @block.tensor
        def _(pe):
            def taken(task, b):
                if task.startswith("max_t"):
                    return qshift_ok, b * 4 + (int(task[-1]) + 1)
                if task.startswith("heads_t"):
                    return attn_ok, b * 2 + (int(task[-1]) + 1)
                if task.startswith("q_stack"):
                    return qs_ok, b * 2 + (int(task[-1]) + 1)
                if task.startswith("k_stack"):
                    return ks_ok, b * 4 + (int(task[-1]) + 1)
                return {"xn_t": xnt_ok, "attn_t": attnt_ok, "q": qlo_ok, "k": klo_ok, "v": v_ok, "wo": x1_ok,
                        "x1_t": x1t_ok, "logits": lg_ok}[task], b + 1

            def misc_bank(task, b):
                if task == "heads_t0" and not isinstance(b, int):
                    return misc[bank_of(task)]
                for n in range(MISC_AT[task] - 2, -2 * len(MISC), -2):
                    before, other = MISC[n % len(MISC)]
                    at = b + (n // len(MISC) + other)
                    if not isinstance(at, int) or 0 <= at < B:
                        pe.wait_ge(*taken(before, at))
                        break
                return misc[bank_of(task)]

            def transpose_xn(b):
                bank = misc_bank("xn_t", b)
                pe.wait_ge(ln_done[0], b * 2 + 4)
                for q in range(QT):
                    last = pe.transpose(bank[:, q * P:(q + 1) * P], xn[:, q, :], ident[:, :])
                last.then_inc(xnt_full, 1)

            def project_q(b):
                bank = misc_bank("q", b)
                pe.wait_ge(xnt_ok, b + 2)
                pe.matmul(bank[:, 0:NQ], wqkvo[:, 0, :], xn_t[:, :], start=True, stop=True).then_inc(q_full, 1)

            def project_k(b, p):
                bank = misc_bank("k", b)
                pe.wait_ge(ld_ctx[p], ctx_count(b + 1, p))
                pe.matmul(bank, wqkvo[:, 1, :], ctx_t[:, p, :], start=True, stop=True).then_inc(k_full, 1)

            def project_v(b, p):
                bank = misc_bank("v", b)
                for kt in range(KT):
                    last = pe.matmul(bank[:, kt * E:(kt + 1) * E], ctx_t[:, p, kt * P:(kt + 1) * P], wqkvo[:, 2, :],
                                     start=True, stop=True)
                last.then_inc(v_full, 1)

            def stack_q(b, n):
                bank = misc_bank(f"q_stack{n}", b)
                pe.wait_ge(qlo_ok, b + 2)
                for s in range(2):
                    out, g = bank[:, s * NQ:(s + 1) * NQ], 2 * n + s
                    pe.matmul(out, sel[:, 0, g, :], q_hi[:, :], start=True, stop=False)
                    last = pe.matmul(out, sel[:, 1, g, :], q_lo[:, :], start=False, stop=True)
                last.then_inc(qs_full, 1)

            def stack_k(b, g):
                bank = misc_bank(f"k_stack{g}", b)
                pe.wait_ge(klo_ok, b + 2)
                pe.matmul(bank, sel[:, 2, g, :], k_hi[:, :], start=True, stop=False)
                pe.matmul(bank, sel[:, 3, g, :], k_lo[:, :], start=False, stop=True).then_inc(ks_full, 1)

            def transpose_heads(b, q):
                bank = misc_bank(f"heads_t{q}", b)
                pe.wait_ge(heads_out, b * 4)
                for g in range(G):
                    last = pe.transpose(bank[:, g * P:(g + 1) * P], out_g[:, g, q * P:(q + 1) * P], ident[:, :])
                last.then_inc(ht_full, 1)

            def transpose_attn(b):
                bank = misc_bank("attn_t", b)
                pe.wait_ge(attn_ok, b * 2)
                for q in range(QT):
                    last = pe.transpose(bank[:, q * P:(q + 1) * P], attn[:, q, :], ident[:, :])
                last.then_inc(at_full, 1)

            def project_o(b):
                bank = misc_bank("wo", b)
                pe.wait_ge(attnt_ok, b)
                for q in range(QT):
                    last = pe.matmul(bank[:, q * E:(q + 1) * E], attn_t[:, q * P:(q + 1) * P], wqkvo[:, 3, :],
                                     start=True, stop=True)
                last.then_inc(wo_full, 1)

            def transpose_x1(b):
                bank = misc_bank("x1_t", b)
                pe.wait_ge(ln_done[1], b * 2)
                for q in range(QT):
                    pe.transpose(bank[:, q * P:(q + 1) * P], xn2[:, q, :], ident[:, :])
                for q in range(QT):
                    last = pe.transpose(bank[:, NQ + q * P:NQ + (q + 1) * P], x1[:, q, :], ident[:, :])
                last.then_inc(x1t_full, 1)

            def route(b):
                bank = misc_bank("logits", b)
                pe.wait_ge(xn2t_ok, b)
                for q in range(QT):
                    last = pe.matmul(bank[:, q * NEXP:(q + 1) * NEXP], xn2_t[:, q * P:(q + 1) * P], rw[:, :],
                                     start=True, stop=True)
                last.then_inc(lg_full, 1)

            def transpose_max(b, g):
                bank = misc_bank(f"max_t{(g + 1) % G}", b)
                pe.wait_ge(negm_ok, b * 4 + (g + 2))
                for q in range(QT):
                    last = pe.transpose(bank[:, q * P:(q + 1) * P], neg_m[:, (g + 1) % 2, q, :], ident[:, :])
                last.then_inc(mt_full, 1)

            def scores(b, p, g, k):
                qt, i = k // HG, k % HG
                if k == 0:
                    pe.wait_ge(pad_ok, b * 4 + (g + 1))
                    if g % 2 == 0:
                        pe.wait_ge(qs_ok, b * 2 + (g // 2 + 1))
                before = {0: -1, 1: 0, 2: -2}.get(k, k - SC + 1)
                wait(pe, max_done, b * 32 + (g * 8 + before))
                pe.matmul(sc[k % SC], q_stack[:, p, g, qt * P:(qt + 1) * P], k_pad[:, p, HG * g + i, :],
                          start=True, stop=True).then_inc(sc_full, 1)

            def scores_t(b, p, g, j):
                kt, pair = j // 2, j % 2
                if j == 0:
                    pe.wait_ge(qshift_ok, b * 4 + (g + 1))
                    if g == 0:
                        pe.wait_ge(mask_ok, b * 2 + 2)
                wait(pe, exp_done, b * 32 + (g * 8 + j - 1))
                pe.matmul(st[j % 2], ident_b[:, :], maskt[:, p, kt, :].unsqueeze(1).to_broadcast([P, 2, NQ]),
                          start=True, stop=False)
                for s in range(2):
                    last = pe.matmul(st[j % 2][:, s * NQ:(s + 1) * NQ],
                                     k_pad[:, p, HG * g + 2 * pair + s, kt * P:(kt + 1) * P], q_shift[:, g % 2, :],
                                     start=False, stop=s == 1)
                last.then_inc(st_full, 1)

            def values(b, p, g, kt):
                if kt == 0:
                    if g == 0:
                        pe.wait_ge(v_ok, b + 1)
                    if isinstance(b, int) and b == 0 and g == 0:
                        pe.wait_ge(tgbo_ok, 1)
                    else:
                        pe.wait_ge(heads_out, b * 4 + g)
                pe.wait_ge(exp_done, b * 32 + (g * 8 + 2 * kt + 2))
                for i in range(HG):
                    last = pe.matmul(ov[R * i:R * (i + 1), :], v_one[:, p, kt, HG * g + i, :],
                                     probs[:, kt, i * NQ:(i + 1) * NQ], start=kt == 0, stop=kt == KT - 1)
                last.then_inc(pv_done, 1)

            SCORES_AT = {0: [0], 1: [1, 2], 2: [3], 3: [4, 5], 4: [6], 5: [7]}

            def slots(b, p, before=None, after=None):
                for g in range(G):
                    last = g == G - 1 and not after
                    for j in range(8):
                        if j == 7 and not last:
                            transpose_max(b, g)
                        scores_t(b, p, g, j)
                        for k in SCORES_AT.get(j, []):
                            if g < G - 1:
                                scores(b, p, g + 1, k)
                            elif after:
                                scores(b + 1, 1 - p, 0, k)
                        if j == 1 and g:
                            values(b, p, g - 1, KT - 1)
                        if j == 1 and not g and before:
                            values(b - 1, 1 - p, G - 1, KT - 1)
                        if j in (3, 5, 7):
                            values(b, p, g, (j - 3) // 2)
                        if g == 0 and before and j in (3, 5):
                            transpose_heads(b, (j - 3) // 2)
                        if g == 1:
                            if j == 0 and after:
                                transpose_xn(b)
                            if j == 1 and before:
                                transpose_attn(b)
                            if j == 2 and after:
                                project_q(b)
                            if j == 3 and after:
                                project_k(b, 1 - p)
                            if j == 4 and after:
                                project_v(b, 1 - p)
                            if j in (5, 6) and after:
                                stack_q(b, j - 5)
                        if g == 2:
                            if j == 0 and before:
                                project_o(b)
                            if 1 <= j <= 4 and after:
                                stack_k(b, j - 1)
                        if g == 3 and before:
                            if j == 1:
                                transpose_x1(b)
                            if j == 3:
                                route(b)

            pe.wait_ge(ld_ident, 16)
            transpose_xn(-1)
            pe.wait_ge(ld_w, 48)
            project_q(-1)
            project_k(-1, 0)
            project_v(-1, 0)
            pe.wait_ge(bvo_ok, 1)
            pe.matmul(banks[:, 5, 0:E], attn[:, 0, :], wqkvo[:, 3, :], start=True, stop=True).then_inc(bvo_full, 1)
            pe.wait_ge(sel_ok, 1)
            stack_q(-1, 0)
            stack_q(-1, 1)
            for g in range(G):
                stack_k(-1, g)
            for k in range(8):
                scores(0, 0, 0, k)
            pe.wait_ge(zeroed_v, 1)
            transpose_max(-1, 3)
            pe.wait_ge(ident_ok, 1)
            pe.wait_ge(zeroed_v, 4)
            slots(0, 0, before=False, after=True)
            pe.wait_ge(ld_c, 48)
            with pe.Fori(1, B - 2, 2) as i:
                slots(i, 1, before=True, after=True)
                slots(i + 1, 0, before=True, after=True)
            slots(B - 1, 1, before=True, after=False)
            values(B - 1, 1, G - 1, KT - 1)
            transpose_heads(B, 0)
            transpose_heads(B, 1)
            transpose_attn(B)
            project_o(B)
            transpose_x1(B)
            route(B)

            def hidden(e, k, p):
                v = e * UNITS_E + k
                mt, half = k // 2, k % 2
                if k == 0:
                    pe.wait_ge(w_lo_ok, e + 1)
                if not (isinstance(e, int) and e == 0 and k < 2):
                    pe.wait_ge(gelu_ok, v - 1)
                w = slice(mt * P, (mt + 1) * P)
                for c in range(2):
                    h = slice(half * HALF + c * CH, half * HALF + (c + 1) * CH)
                    pe.matmul(hid[k % 2][:, c, :], w_hi[p][:, w], h_lo[:, h], start=True, stop=False)
                    pe.matmul(hid[k % 2][:, c, :], w_lo[p][:, w], h_hi[:, h], start=False, stop=False)
                    last = pe.matmul(hid[k % 2][:, c, :], w_hi[p][:, w], h_hi[:, h], start=False, stop=True)
                last.then_inc(hid_full, 1)

            def output(e, k, p):
                v = e * UNITS_E + k
                mt, half = k // 2, k % 2
                pe.wait_ge(g_lo_ok, v + 1)
                w = slice(FF + mt * E, FF + (mt + 1) * E)
                for c in range(2):
                    g, out = slice(c * CH, (c + 1) * CH), acc[2 * half + c]
                    for wt, gt in ((w_hi, g_lo), (w_lo, g_hi), (w_hi, g_hi)):
                        last = pe.matmul(out, wt[p][:, w], gt[k % 2][:, g], start=False, stop=True, skip_group_check=True)
                last.then_inc(ff_done, 1)

            def expert(e, p, final=False):
                for k in range(UNITS_E):
                    if k + AHEAD < UNITS_E:
                        hidden(e, k + AHEAD, p)
                    elif not final:
                        hidden(e + 1, k + AHEAD - UNITS_E, 1 - p)
                    output(e, k, p)

            pe.wait_ge(hlo_ok, B)
            hidden(0, 0, 0)
            hidden(0, 1, 0)
            pe.wait_ge(cw_ok, 1)
            pe.wait_ge(x1t_ok, B)
            for c in range(4):
                for n in range(4):
                    last = pe.transpose(acc[c][0:NEXP, n * P:(n + 1) * P], rt[:, 1, 4 * c + n, :], ident[:, :])
                last.then_inc(cwt_full, 1)
            for c in range(4):
                pe.wait_ge(cwt_ok, c + 1)
                pe.matmul(acc[c], b2[:, :], cw_t[:, c * CH:(c + 1) * CH], start=True, stop=True)
            for k in range(2, AHEAD):
                hidden(0, k, 0)
            with pe.Fori(0, NEXP - 3, 2) as i:
                expert(i, 0)
                expert(i + 1, 1)
            expert(NEXP - 2, 0)
            expert(NEXP - 1, 1, final=True)


def kernel(x, ctx_1024, mask_BxSxS2_bf1, g_xattn, g_ffn, L0_xattn_Wq, L0_xattn_bq, L0_xattn_Wk, L0_xattn_bk,
           L0_xattn_Wv, L0_xattn_bv, L0_xattn_Wo, L0_xattn_bo, L0_ffn_router_w, L0_ffn_router_b, L0_ffn_w1,
           L0_ffn_b1, L0_ffn_w2, L0_ffn_b2):
    import concourse.bacc as bacc
    from concourse.bass_utils import run_bass_kernel_spmd

    def arr(a):
        return np.asarray(a)

    mask = arr(mask_BxSxS2_bf1).view(np.uint8)
    sel, ones = stack_selectors()
    notfirst = np.ones((TT, NEXP), np.float32)
    notfirst[:, 0] = 0.0
    w1 = arr(L0_ffn_w1)
    w2 = arr(L0_ffn_w2).reshape(NEXP, MT, P, E).transpose(0, 2, 1, 3).reshape(NEXP, P, MT * E)
    b1 = arr(L0_ffn_b1).reshape(NEXP, MT, P).transpose(0, 2, 1)
    arrays = {
        "x": arr(x).reshape(TOK, E),
        "ctx_t": arr(ctx_1024).transpose(0, 2, 1),
        "maskq": mask,
        "maskt": mask.transpose(0, 2, 1),
        "wqkvo": np.concatenate([arr(w).T for w in (L0_xattn_Wq, L0_xattn_Wk, L0_xattn_Wv, L0_xattn_Wo)], axis=1),
        "cols": np.stack([arr(L0_xattn_bq), arr(L0_xattn_bk), ones[:, 0], arr(L0_xattn_bv)], axis=1),
        "rows": np.concatenate([arr(a).reshape(1, -1) for a in (L0_xattn_bo, L0_ffn_router_b, g_xattn,
                                                                 g_ffn)], axis=1),
        "ident": np.eye(P, dtype=np.float32),
        "sel": sel,
        "notfirst": notfirst.reshape(1, -1),
        "router_w": arr(L0_ffn_router_w),
        "b2": arr(L0_ffn_b2),
        "experts": np.concatenate([w1, w2, b1], axis=2),
    }
    arrays = {k: np.ascontiguousarray(a) for k, a in arrays.items()}
    nc = bacc.Bacc("TRN2", target_bir_lowering=False, num_devices=1)
    tensors = {k: nc.dram_tensor("in_" + k, a.shape, mybir.dt.from_np(a.dtype), kind="ExternalInput").ap()
               for k, a in arrays.items()}
    tensors["cw"] = nc.dram_tensor("expert_weights", (NEXP, TOK), F32, kind="Internal").ap()
    tensors["out"] = nc.dram_tensor("out", (E, TOK), F32, kind="ExternalOutput").ap()
    build(nc, tensors)
    r = run_bass_kernel_spmd(nc, [{"in_" + k: a for k, a in arrays.items()}], core_ids=[0])
    return np.ascontiguousarray(r.results[0]["out"].T).reshape(B, NQ, E)
```

```python
from contextlib import ExitStack

import numpy as np

import concourse.bass as bass
from concourse import mybir

F32 = mybir.dt.float32
F32R = mybir.dt.float32r
BF16 = mybir.dt.bfloat16
I32 = mybir.dt.int32
ALU = mybir.AluOpType
ACT = mybir.ActivationFunctionType
AX_X = mybir.AxisListType.X

B, NQ, NK, E = 8, 256, 512, 128
H, D = 16, 8
P = 128
QT, KT = NQ // P, NK // P
G, HG = 4, 4
R = 32
NEXP, TOPK, FF = 16, 4, 256
MT = FF // P
TOK = B * NQ
TT = TOK // P
CH = 512
SC = 3
EARLY = 13
UNITS_E = MT * 2
AHEAD = 3
SCALE = float(D) ** -0.5
EPS = 1e-5
MASKED = 1e30
LN_STEPS = 2 * QT + 2 + 9
GUESS = float(0x5F3759DF - 2 ** 30 - 2 ** 22)


def stack_selectors():
    sel = np.zeros((P, 4, G, P), np.float32)
    for g in range(G):
        for i in range(HG):
            for d in range(D):
                f, r = (g * HG + i) * D + d, i * R + 2 + d
                for matrix, block in ((0, 0), (0, 1), (1, 2), (2, 0), (3, 1), (2, 2)):
                    sel[f, matrix, g, r + block * D] = 1.0
    ones = np.zeros((P, 1), np.float32)
    for i in range(HG):
        ones[i * R:i * R + 2] = 1.0
    return sel.reshape(P, 4 * G * P), ones


def build(nc, t):
    ctx = ExitStack()
    with ctx:
        def sb(name, shape, dt=F32):
            return ctx.enter_context(nc.sbuf_tensor(name, shape, dt))

        def sem(name):
            return ctx.enter_context(nc.semaphore(name))

        wqkvo = sb("wqkvo", [P, 4, E])
        cols = sb("cols", [P, 4])
        rows = sb("rows", [P, E + NEXP + 2])
        rb_row = rows[:, E:E + NEXP]
        gates = rows[:, E + NEXP:]
        ident = sb("ident", [P, P])
        ident_b = sb("ident_b", [P, P], BF16)
        sel = sb("sel", [P, 4, G, P], F32R)
        notfirst = sb("notfirst", [P, TT * NEXP])
        rw = sb("rw", [P, NEXP])
        b2 = sb("b2", [NEXP, E])
        tgates = sb("tgates", [P, 2])
        tg_bo = sb("tg_bo", [P, E])

        x_sb = sb("x_sb", [P, TT, E])
        ctx_t = sb("ctx_t", [P, 2, NK])
        xn = sb("xn", [P, QT, E])
        xn_t = sb("xn_t", [P, NQ])
        q_hi, q_lo = sb("q_hi", [P, NQ], F32R), sb("q_lo", [P, NQ], F32R)
        k_hi, k_lo = sb("k_hi", [P, NK], F32R), sb("k_lo", [P, NK], F32R)
        k_stack = sb("k_stack", [P, 2, NK])
        k_pad = sb("k_pad", [P, 2, H, NK], F32R)
        q_stack = sb("q_stack", [P, 2, G, NQ], F32R)
        q_shift = sb("q_shift", [P, 2, NQ], F32R)
        v_one = sb("v_one", [P, 2, KT, H, R])
        probs = sb("probs", [P, KT, HG * NQ])
        selraw = probs[:, 0:2, :].rearrange("p t n -> p (t n)")
        maskq_u8 = sb("maskq_u8", [P, QT, NK], mybir.dt.uint8)
        maskt_u8 = sb("maskt_u8", [P, KT, NQ], mybir.dt.uint8)
        maskq = sb("maskq", [P, 2, QT, NK], BF16)
        maskt = sb("maskt", [P, 2, KT, NQ], BF16)
        mask_sum = sb("mask_sum", [P, 2])
        all_kept = sb("all_kept", [1, 2], I32)
        minus_masked = sb("minus_masked", [P, 1])
        ones, zero = sb("ones", [P, 1]), sb("zero", [P, 1])
        maxes = sb("maxes", [P, 2, QT, H])
        neg_m = sb("neg_m", [P, 2, QT, P])
        out_g = sb("out_g", [P, G, NQ])
        dead = sb("dead", [P, 3, QT])
        inv = sb("inv", [P, 2, H])
        attn = sb("attn", [P, QT, E])
        attn_t = sb("attn_t", [P, NQ])
        x_bo = sb("x_bo", [P, QT, E])
        x1 = sb("x1", [P, QT, E])
        xn2 = sb("xn2", [P, QT, E])
        xn2_t = sb("xn2_t", [P, NQ])
        stats = sb("stats", [P, 2, TT, 6])
        meanvar = sb("meanvar", [P, 2, TT, 2])
        rstd = sb("rstd", [P, 2, 3, TT])
        x1_t = sb("x1_t", [P, TOK])
        h_hi, h_lo = sb("h_hi", [P, TOK], F32R), sb("h_lo", [P, TOK], F32R)
        logits = sb("logits", [P, TT, NEXP])
        top8 = sb("top8", [P, TT, 8])
        rt = sb("rt", [P, 4, TT, NEXP])
        rs = sb("rs", [P, 4, TT])
        cw_t = x_sb[0:NEXP, :, :].rearrange("p t f -> p (t f)")

        banks = ctx.enter_context(nc.psum_tensor("banks", [P, 8, CH], F32))
        sc = [banks[:, n, :] for n in range(SC)]
        st = [banks[:, 3, :], banks[:, 4, :]]
        ov = banks[:, 5, 0:NQ]
        misc = [banks[:, 6, :], banks[:, 7, :]]
        hid = [banks[:, 0:2, :], banks[:, 2:4, :]]
        acc = [banks[:, 4 + c, :] for c in range(4)]

        MISC = [("k", 1, 0), ("v", 1, 1), ("xn_t", 1, 1), ("max_t1", 0, 0), ("heads_t0", -1, 1), ("q", 1, 0),
                ("heads_t1", -1, 1), ("attn_t", -1, 1), ("max_t2", 0, 0), ("k_stack0", 1, 1), ("wo", -1, 1),
                ("q_stack0", 1, 0), ("k_stack1", 1, 0), ("k_stack2", 1, 1), ("max_t3", 0, 0), ("k_stack3", 1, 1),
                ("q_stack1", 1, 0), ("x1_t", -1, 1), ("logits", -1, 1), ("max_t0", 1, 0)]
        MISC_AT = {task: n for n, (task, _, _) in enumerate(MISC)}

        def scores_at(b, p, g, j):
            over, n = divmod(g * 8 + j + EARLY, G * 8)
            return b + over, (p + over) % 2, n // 8, n % 8, over

        def bank_of(task):
            return MISC[MISC_AT[task]][2]

        ld_x0, ld_x, ld_w, ld_cols, ld_rows, ld_ident, ld_c, ld_sel = (sem(n) for n in (
            "ld_x0", "ld_x", "ld_w", "ld_cols", "ld_rows", "ld_ident", "ld_c", "ld_sel"))
        ld_ctx = [sem("ld_ctx0"), sem("ld_ctx1")]
        ld_mask = sem("ld_mask")
        ld_exp = [sem("ld_exp0"), sem("ld_exp1")]
        st_cw, st_out = sem("st_cw"), sem("st_out")
        ld_cw = [sem("ld_cw0"), sem("ld_cw1")]
        ident_ok, zeroed_v, zeroed_v1, sel_ok, tanh_ok, bvo_full, bvo_ok, tgbo_ok = (sem(n) for n in (
            "ident_ok", "zeroed_v", "zeroed_v1", "sel_ok", "tanh_ok", "bvo_full", "bvo_ok", "tgbo_ok"))
        zeroed = [sem("zeroed0"), sem("zeroed1")]
        xnt_full, q_full, k_full, v_full, qs_full, ks_full, mt_full, ht_full, at_full, wo_full, x1t_full, lg_full = (
            sem(n + "_full") for n in ("xnt", "q", "k", "v", "qs", "ks", "mt", "ht", "at", "wo", "x1t", "lg"))
        sc_full, max_done, st_full, exp_done, pv_done, heads_out = (sem(n) for n in (
            "sc_full", "max_done", "st_full", "exp_done", "pv_done", "heads_out"))
        ln_done = [sem("ln1_done"), sem("ln2_done")]
        ln_step = [sem("ln1_step"), sem("ln2_step")]
        xnt_ok, qhi_ok, qlo_ok, khi_ok, klo_ok, v_ok, qs_ok, ks_ok, pad_ok, maskq_ok, maskt_ok, flag_ok = (sem(n) for n in (
            "xnt_ok", "qhi_ok", "qlo_ok", "khi_ok", "klo_ok", "v_ok", "qs_ok", "ks_ok", "pad_ok", "maskq_ok", "maskt_ok",
            "flag_ok"))
        negm_hi, negm_ok, qshift_ok, norm_step, attn_ok, attnt_ok, xbo_step, xbo_ok, x1_ok, xn2t_ok, x1t_ok, hhi_ok, hlo_ok, lg_ok = (
            sem(n) for n in ("negm_hi", "negm_ok", "qshift_ok", "norm_step", "attn_ok", "attnt_ok", "xbo_step", "xbo_ok",
                             "x1_ok", "xn2t_ok", "x1t_ok", "hhi_ok", "hlo_ok", "lg_ok"))
        rt_step, z_ok, rexp_ok, cw_ok, cwt_full, cwt_ok = (sem(n) for n in (
            "rt_step", "z_ok", "rexp_ok", "cw_ok", "cwt_full", "cwt_ok"))
        w_hi_ok, w_lo_ok, hid_full, gelu_ok, gw_ok, g_hi_ok, g_lo_ok, ff_done, out_ok = (sem(n) for n in (
            "w_hi_ok", "w_lo_ok", "hid_full", "gelu_ok", "gw_ok", "g_hi_ok", "g_lo_ok", "ff_done", "out_ok"))

        WCOLS = FF + MT * E
        HALF = 2 * CH
        w_raw = sb("w_raw", [P, 2, WCOLS + MT])
        under = k_pad[:, 0, :, :].rearrange("p h n -> p (h n)")
        w_hi = [under[:, n * WCOLS:(n + 1) * WCOLS] for n in (0, 1)]
        w_lo = [under[:, n * WCOLS:(n + 1) * WCOLS] for n in (2, 3)]
        g_hi = [under[:, n * HALF:(n + 1) * HALF] for n in (2, 3)]
        g_lo = [under[:, n * HALF:(n + 1) * HALF] for n in (4, 5)]
        gel = [probs[:, n, :] for n in (0, 1)]
        gw = [probs[:, n, :] for n in (2, 3)]
        under = v_one[:, :, :, :, :].rearrange("p a t h r -> p (a t h r)")
        cw = [under[:, n * TOK:(n + 1) * TOK] for n in (0, 1)]

        block = ctx.enter_context(nc.Block())

        def wait(eng, s, n):
            if not (isinstance(n, int) and n <= 0):
                eng.wait_ge(s, n)

        def wait_apart(eng, s, n):
            n = n if isinstance(n, int) else eng.to_reg(n)
            eng.wait_ge(ld_x0, 16)
            eng.wait_ge(s, n)

        def ctx_count(b, p):
            return b * 8 + (16 if p == 0 else 8)

        @block.sync
        def _(sp):
            sp.dma_start(wqkvo[:, :, :], t["wqkvo"].rearrange("p (m f) -> p m f", m=4)).then_inc(ld_w, 16)
            sp.dma_start(ctx_t[:, 0, :], t["ctx_t"][0]).then_inc(ld_ctx[0], 16)
            sp.dma_start(selraw, t["sel"]).then_inc(ld_sel, 16)
            sp.dma_start(maskq_u8[:, :, :], t["maskq"][0].rearrange("(t p) k -> p t k", p=P)).then_inc(ld_mask, 16)
            sp.dma_start(maskt_u8[:, :, :], t["maskt"][0].rearrange("(t p) q -> p t q", p=P)).then_inc(ld_mask, 16)
            sp.dma_start(x_sb[:, 2 * QT:, :], t["x"][2 * NQ:, :].rearrange("(t p) f -> p t f", p=P)).then_inc(ld_x, 16)
            sp.dma_start(ctx_t[:, 1, :], t["ctx_t"][1]).then_inc(ld_ctx[1], 16)
            sp.dma_start(notfirst[:, :], t["notfirst"].partition_broadcast(P)).then_inc(ld_c, 16)
            sp.dma_start(rw[:, :], t["router_w"]).then_inc(ld_c, 16)
            sp.dma_start(b2[:, :], t["b2"]).then_inc(ld_c, 16)
            for e in range(2):
                sp.dma_start(w_raw[:, e, :], t["experts"][e]).then_inc(ld_exp[e], 16)

            def masks(b):
                wait_apart(sp, maskq_ok, b)
                wait_apart(sp, maskt_ok, b)
                sp.dma_start(maskq_u8[:, :, :], t["maskq"][b].rearrange("(t p) k -> p t k", p=P)).then_inc(ld_mask, 16)
                sp.dma_start(maskt_u8[:, :, :], t["maskt"][b].rearrange("(t p) q -> p t q", p=P)).then_inc(ld_mask, 16)

            masks(1)
            with sp.Fori(0, B - 3, 2) as i:
                for p in range(2):
                    b = i + p
                    wait_apart(sp, v_full, b + 1)
                    sp.dma_start(ctx_t[:, p, :], t["ctx_t"][b + 2]).then_inc(ld_ctx[p], 16)
                    masks(b + 2)
            sp.wait_ge(cwt_ok, 4)
            sp.dma_start(t["cw"], cw_t[:, :]).then_inc(st_cw, 16)
            sp.wait_ge(st_cw, 16)
            for e in range(2):
                sp.dma_start(cw[e], t["cw"][e:e + 1, :].partition_broadcast(P)).then_inc(ld_cw[e], 16)

            def next_expert(e, p):
                wait_apart(sp, ff_done, e * UNITS_E + 2)
                wait_apart(sp, gelu_ok, e * UNITS_E + UNITS_E)
                sp.dma_start(w_raw[:, p, :], t["experts"][e + 2]).then_inc(ld_exp[p], 16)
                wait_apart(sp, gw_ok, e * UNITS_E + UNITS_E)
                sp.dma_start(cw[p], t["cw"][bass.ds(e + 2, 1), :].partition_broadcast(P)).then_inc(ld_cw[p], 16)

            with sp.Fori(0, NEXP - 3, 2) as i:
                for p in range(2):
                    next_expert(i + p, p)
            for c in range(4):
                sp.wait_ge(out_ok, c + 1)
                sp.dma_start(t["out"][:, c * CH:(c + 1) * CH], x1_t[:, c * CH:(c + 1) * CH]).then_inc(st_out, 16)
            sp.wait_ge(st_out, 4 * 16)

        @block.gpsimd
        def _(pool):
            def mask_bias(b, p):
                wait_apart(pool, ld_mask, b * 32 + 32)
                if not isinstance(b, int) or b >= 2:
                    wait_apart(pool, max_done, b * 32 - 32)
                pool.tensor_scalar(maskq[:, p, :, :], maskq_u8[:, :, :], -1.0, MASKED, ALU.add, ALU.mult).then_inc(maskq_ok, 1)

            def x_plus_bo(b, p):
                if isinstance(b, int) and b == 0:
                    pool.wait_ge(tgbo_ok, 1)
                bo = tg_bo[:, :].unsqueeze(1).to_broadcast([P, QT, E])
                pool.tensor_tensor(x_bo[:, :, :], x_sb[:, bass.ds(b * QT, QT), :], bo, ALU.add).then_inc(xbo_step, 1)
                m = maxes[:, p, :, 0]
                wait_apart(pool, max_done, b * 32 + 8)
                pool.tensor_scalar(dead[:, 0, :], m, -1.0, -MASKED / 2, ALU.mult, ALU.add).then_inc(xbo_step, 1)
                wait_apart(pool, xbo_step, b * 4 + 2)
                pool.tensor_scalar(dead[:, 1, :], dead[:, 0, :], 0.0, MASKED, ALU.max, ALU.mult).then_inc(xbo_step, 1)
                wait_apart(pool, xbo_step, b * 4 + 3)
                pool.tensor_scalar(dead[:, 2, :], dead[:, 1, :], 0.0, None, ALU.mult).then_inc(xbo_step, 1)
                wait_apart(pool, xbo_step, b * 4 + 4)
                pool.tensor_tensor(x_bo[:, :, :], x_bo[:, :, :], dead[:, 2, :].unsqueeze(2).to_broadcast([P, QT, E]),
                                   ALU.add).then_inc(xbo_ok, 1)

            def h_halves(b):
                wait_apart(pool, xn2t_ok, b + 1)
                cols_b = bass.ds(b * NQ, NQ)
                pool.tensor_copy(h_hi[:, cols_b], xn2_t[:, :]).then_inc(hhi_ok, 1)
                wait_apart(pool, hhi_ok, b + 1)
                pool.tensor_tensor(h_lo[:, cols_b], xn2_t[:, :], h_hi[:, cols_b].bitcast(F32), ALU.subtract).then_inc(hlo_ok, 1)

            def pad(b, p, g):
                if g == 0:
                    pool.wait_ge(maskq_ok, b + 1)
                wait_apart(pool, ks_ok, b * G + g + 1)
                if isinstance(b, int) and b < 2:
                    pool.wait_ge(zeroed[p], g + 1)
                for i in range(HG):
                    last = pool.tensor_scalar(k_pad[R * i:R * (i + 1), p, HG * g + i, :], k_stack[R * i:R * (i + 1), g % 2, :],
                                              1.0, 0.0, ALU.mult, ALU.add)
                last.then_inc(pad_ok, 1)

            def batch(b, p):
                mask_bias(b, p)
                for g in range(G):
                    pad(b, p, g)
                wait_apart(pool, pad_ok, b * G + G)
                if not isinstance(b, int) or b >= 2:
                    h_halves(b - 2)
                x_plus_bo(b - 1, 1 - p)

            for g in range(G):
                pool.memset(k_pad[:, 0, HG * g:HG * (g + 1), :].bitcast(F32), 0.0).then_inc(zeroed[0], 1)
            pool.memset(v_one[:, 1, :, :, :], 0.0).then_inc(zeroed_v1, 1)
            pool.wait_ge(zeroed_v1, 1)
            pool.memset(v_one[:, 1, :, :, D:D + 1].rearrange("p t h r -> p (t h) r"), 1.0).then_inc(zeroed_v1, 1)
            mask_bias(0, 0)
            for g in range(G):
                pad(0, 0, g)
            pool.wait_ge(pad_ok, G)
            pool.wait_ge(ld_x, 16)
            batch(1, 1)
            with pool.Fori(2, B - 1, 2) as i:
                batch(i, 0)
                batch(i + 1, 1)
            h_halves(B - 2)
            x_plus_bo(B - 1, 1)
            h_halves(B - 1)

            def weight_halves(e, p):
                pool.wait_ge(ld_exp[p], e * 8 + (16 if p == 0 else 8))
                if isinstance(e, int) and e < 2:
                    pool.wait_ge(exp_done, B * 32)
                else:
                    wait_apart(pool, ff_done, e * UNITS_E - UNITS_E)
                pool.tensor_scalar(w_hi[p], w_raw[:, p, 0:WCOLS], 1.0, 0.0, ALU.mult, ALU.add).then_inc(w_hi_ok, 1)
                pool.wait_ge(w_hi_ok, e + 1)
                pool.tensor_tensor(w_lo[p], w_raw[:, p, 0:WCOLS], w_hi[p].bitcast(F32), ALU.subtract).then_inc(w_lo_ok, 1)

            weight_halves(0, 0)
            weight_halves(1, 1)
            with pool.Fori(2, NEXP - 1, 2) as i:
                weight_halves(i, 0)
                weight_halves(i + 1, 1)

        @block.scalar
        def _(act):
            def xn_t_copy(b):
                act.wait_ge(xnt_full, b + 1)
                act.activation(xn_t[:, :], misc[bank_of("xn_t")][:, 0:NQ], ACT.Copy).then_inc(xnt_ok, 1)

            def q_hi_half(b):
                act.wait_ge(q_full, b + 1)
                wait(act, qs_full, b * 2)
                act.activation(q_hi[:, :], misc[bank_of("q")][:, 0:NQ], ACT.Identity, bias=cols[:, 0:1]).then_inc(qhi_ok, 1)

            def k_hi_half(b):
                act.wait_ge(k_full, b + 1)
                wait(act, ks_full, b * G)
                act.activation(k_hi[:, :], misc[bank_of("k")], ACT.Identity, bias=cols[:, 1:2]).then_inc(khi_ok, 1)

            def q_stack_out(b, p, n):
                act.wait_ge(qs_full, b * 2 + n + 1)
                bank = bank_of(f"q_stack{n}")
                act.activation(q_stack[:, p, 2 * n:2 * n + 2, :].rearrange("p g q -> p (g q)"), misc[bank],
                               ACT.Copy).then_inc(qs_ok, 1)

            def k_stack_out(b, g):
                act.wait_ge(ks_full, b * G + g + 1)
                if not (isinstance(b, int) and b == 0 and g < 2):
                    act.wait_ge(pad_ok, b * G + g - 1)
                bank = bank_of(f"k_stack{g}")
                act.activation(k_stack[:, g % 2, :], misc[bank], ACT.Identity, bias=cols[:, 2:3]).then_inc(ks_ok, 1)

            def mask_bias_t(b, p):
                act.wait_ge(ld_mask, b * 32 + 32)
                act.activation(maskt[:, p, :, :].rearrange("p t q -> p (t q)"), maskt_u8[:, :, :].rearrange("p t q -> p (t q)"),
                               ACT.Identity, scale=MASKED, bias=minus_masked[:, :],
                               accum_out=mask_sum[:, p:p + 1]).then_inc(maskt_ok, 1)

            def v_out(b, p):
                act.wait_ge(v_full, b + 1)
                if not isinstance(b, int) or b >= 2:
                    act.wait_ge(pv_done, b * 16 - 16)
                act.activation(v_one[:, p, :, :, 0:D].rearrange("p t h d -> p (t h) d"),
                               misc[bank_of("v")].rearrange("p (h d) -> p h d", d=D), ACT.Copy).then_inc(v_ok, 1)

            def exp(b, g, j):
                kt, pair = j // 2, j % 2
                act.wait_ge(st_full, b * 32 + g * 8 + j + 1)
                if pair == 0:
                    wait(act, pv_done, b * 16 + g * 4 - 3 + kt)
                act.activation(probs[:, kt, pair * CH:(pair + 1) * CH], st[j % 2], ACT.Exp, scale=SCALE).then_inc(exp_done, 1)

            def heads_copy(b, g):
                act.wait_ge(pv_done, b * 16 + g * 4 + 4)
                act.activation(out_g[:, g, :], ov, ACT.Copy).then_inc(heads_out, 1)

            def attn_t_copy(b):
                act.wait_ge(at_full, b + 1)
                bank = bank_of("attn_t")
                act.activation(attn_t[:, :], misc[bank][:, 0:NQ], ACT.Copy).then_inc(attnt_ok, 1)

            def x1_t_copy(b):
                act.wait_ge(x1t_full, b + 1)
                bank = bank_of("x1_t")
                act.activation(xn2_t[:, :], misc[bank][:, 0:NQ], ACT.Copy).then_inc(xn2t_ok, 1)
                act.activation(x1_t[:, bass.ds(b * NQ, NQ)], misc[bank][:, NQ:], ACT.Copy).then_inc(x1t_ok, 1)

            def slots(b, p, before=None, after=None):
                for g in range(G):
                    for j in range(8):
                        exp(b, g, j)
                        if j == 1 and (before or g):
                            if g:
                                heads_copy(b, g - 1)
                            else:
                                heads_copy(b - 1, G - 1)
                        step = g * 8 + j
                        if after:
                            if step == 1:
                                k_hi_half(b + 1)
                            if step == 2:
                                v_out(b + 1, 1 - p)
                            if step == 4:
                                xn_t_copy(b + 1)
                            if step == 6:
                                mask_bias_t(b + 1, 1 - p)
                            if step == 9:
                                q_hi_half(b + 1)
                            if step in (14, 19, 20, 23):
                                k_stack_out(b + 1, (14, 19, 20, 23).index(step))
                            if step in (17, 25):
                                q_stack_out(b + 1, 1 - p, (17, 25).index(step))
                        if before:
                            if step == 12:
                                attn_t_copy(b - 1)
                            if step == 27:
                                x1_t_copy(b - 1)

            act.dma_start(x_sb[:, 0:2 * QT, :], t["x"][0:2 * NQ, :].rearrange("(t p) f -> p t f", p=P)).then_inc(ld_x0, 16)
            act.dma_start(cols[:, :], t["cols"]).then_inc(ld_cols, 16)
            act.dma_start(ident[:, :], t["ident"]).then_inc(ld_ident, 16)
            act.dma_start(rows[:, :], t["rows"].partition_broadcast(P)).then_inc(ld_rows, 16)
            def zero_pad(g):
                act.activation(k_pad[:, 1, HG * g:HG * (g + 1), :].rearrange("p h n -> p (h n)"),
                               zero[:, :].to_broadcast([P, HG * NK]), ACT.Copy).then_inc(zeroed[1], 1)

            act.wait_ge(zeroed_v, 1)
            zero_pad(0)
            act.wait_ge(ld_cols, 16)
            k_hi_half(0)
            act.wait_ge(zeroed_v, 3)
            v_out(0, 0)
            xn_t_copy(0)
            q_hi_half(0)
            act.wait_ge(ld_rows, 16)
            act.activation(tgates[:, :], gates, ACT.Tanh).then_inc(tanh_ok, 1)
            k_stack_out(0, 0)
            q_stack_out(0, 0, 0)
            mask_bias_t(0, 0)
            for g in range(1, G):
                k_stack_out(0, g)
                if g == G - 1:
                    q_stack_out(0, 0, 1)
                zero_pad(g)
            act.wait_ge(zeroed_v1, 2)
            slots(0, 0, before=False, after=True)
            with act.Fori(1, B - 2, 2) as i:
                slots(i, 1, before=True, after=True)
                slots(i + 1, 0, before=True, after=True)
            slots(B - 1, 1, before=True, after=False)
            heads_copy(B - 1, G - 1)
            attn_t_copy(B - 1)
            x1_t_copy(B - 1)

            act.wait_ge(z_ok, 1)
            act.activation(rt[:, 1, :, :], rt[:, 0, :, :], ACT.Exp).then_inc(rexp_ok, 1)

            def gelu(e, k, p):
                v = e * UNITS_E + k
                act.wait_ge(hid_full, v + 1)
                wait(act, gw_ok, v - 1)
                mt = k // 2
                act.activation(gel[k % 2], hid[k % 2].rearrange("p a c -> p (a c)"), ACT.Gelu,
                               bias=w_raw[:, p, WCOLS + mt:WCOLS + mt + 1]).then_inc(gelu_ok, 1)

            def hi_half(v, par):
                act.wait_ge(gw_ok, v + 1)
                wait(act, ff_done, v - 1)
                act.activation(g_hi[par], gw[par], ACT.Copy).then_inc(g_hi_ok, 1)

            def expert(e, p, first=False):
                for k in range(UNITS_E):
                    gelu(e, k, p)
                    if not (first and k == 0):
                        hi_half(e * UNITS_E + k - 1, (k - 1) % 2)

            expert(0, 0, first=True)
            expert(1, 1)
            with act.Fori(2, NEXP - 1, 2) as i:
                expert(i, 0)
                expert(i + 1, 1)
            hi_half(NEXP * UNITS_E - 1, 1)

        @block.vector
        def _(dve):
            def statistics(n, base, src, at, step):
                half, y, tmp = (rstd[:, n, k, at] for k in range(3))
                if step == 0:
                    for q, tile in enumerate(src):
                        dve.bn_stats(stats[:, n, at.start + q, :], tile).then_inc(ln_step[n], 1)
                    return
                if step == 1:
                    wait_apart(dve, ln_step[n], base + len(src))
                    for q in range(len(src)):
                        dve.bn_aggr(meanvar[:, n, at.start + q, :], stats[:, n, at.start + q, :]).then_inc(ln_step[n], 1)
                    return
                dve.wait_ge(ln_step[n], base + (2 * len(src) + step - 2))
                if step == 2:
                    ins = dve.tensor_scalar(half, meanvar[:, n, at, 1], EPS, -0.5, ALU.add, ALU.mult)
                elif step == 3:
                    ins = dve.tensor_scalar(y.bitcast(I32), half.bitcast(I32), -0.5, GUESS, ALU.mult, ALU.add)
                elif step % 3 == 1:
                    ins = dve.tensor_tensor(tmp, y, y, ALU.mult)
                elif step % 3 == 2:
                    ins = dve.tensor_tensor(tmp, tmp, half, ALU.mult)
                else:
                    ins = dve.scalar_tensor_tensor(out=y, in0=tmp, scalar=1.5, in1=y, op0=ALU.add, op1=ALU.mult)
                ins.then_inc(ln_step[n], 1)

            def ln_x_statistics(tiles, count, *steps):
                for step in steps:
                    statistics(0, count, [x_sb[:, n, :] for n in range(tiles.start, tiles.stop)], tiles, step)
                if steps[-1] == 12:
                    dve.wait_ge(ln_step[0], count + 2 * (tiles.stop - tiles.start) + 11)

            def ln_x(b):
                for q in range(QT):
                    n = b * QT + q
                    n = slice(n, n + 1) if isinstance(n, int) else bass.ds(n, 1)
                    dve.tensor_scalar(xn[:, q, :], x_sb[:, n, :].rearrange("p t f -> p (t f)"), meanvar[:, 0, n, 0],
                                      rstd[:, 0, 1, n], ALU.subtract, ALU.mult).then_inc(ln_done[0], 1)

            def ln_x1_statistics(b, *steps):
                for step in steps:
                    if step == 0:
                        dve.wait_ge(x1_ok, b + 1)
                    statistics(1, b * LN_STEPS, [x1[:, q, :] for q in range(QT)], slice(0, QT), step)

            def ln_x1(b):
                dve.wait_ge(ln_step[1], b * LN_STEPS + LN_STEPS)
                for q in range(QT):
                    dve.tensor_scalar(xn2[:, q, :], x1[:, q, :], meanvar[:, 1, q, 0:1], rstd[:, 1, 1, q:q + 1],
                                      ALU.subtract, ALU.mult).then_inc(ln_done[1], 1)

            def q_lo_half(b):
                dve.wait_ge(qhi_ok, b + 1)
                dve.scalar_tensor_tensor(out=q_lo[:, :], in0=misc[bank_of("q")][:, 0:NQ], scalar=cols[:, 0:1],
                                         in1=q_hi[:, :].bitcast(F32), op0=ALU.add, op1=ALU.subtract).then_inc(qlo_ok, 1)

            def k_lo_half(b):
                dve.wait_ge(khi_ok, b + 1)
                dve.scalar_tensor_tensor(out=k_lo[:, :], in0=misc[bank_of("k")], scalar=cols[:, 1:2],
                                         in1=k_hi[:, :].bitcast(F32), op0=ALU.add, op1=ALU.subtract).then_inc(klo_ok, 1)

            def row_max(b, p, g, k):
                qt, i = k // HG, k % HG
                if g == 0 and k == 0:
                    dve.wait_ge(maskq_ok, b + 1)
                wait_apart(dve, sc_full, b * 32 + (g * 8 + k + 1))
                h = HG * g + i
                dve.tensor_tensor_reduce(sc[k % SC], sc[k % SC], maskq[:, p, qt, :], 1.0, -3.0e38, ALU.add, ALU.max,
                                         maxes[:, p, qt, h:h + 1]).then_inc(max_done, 1)

            def minus_max(b, p, g):
                dve.wait_ge(max_done, b * 32 + (g * 8 + 8))
                if not (isinstance(b, int) and b == 0 and g < 2):
                    dve.wait_ge(mt_full, b * 4 + (g - 1))
                m = maxes[:, p, :, HG * g:HG * (g + 1)]
                col = neg_m[:, g % 2, :, :].rearrange("p q (i r) -> p q i r", r=R)
                dve.tensor_scalar(col[:, :, :, 0].bitcast(F32R), m, -1.0, None, ALU.mult).then_inc(negm_hi, 1)
                dve.wait_ge(negm_hi, b * 4 + (g + 1))
                dve.scalar_tensor_tensor(out=col[:, :, :, 1], in0=m, scalar=-1.0, in1=col[:, :, :, 0], op0=ALU.mult,
                                         op1=ALU.subtract).then_inc(negm_ok, 1)

            def shift(b, p, g, flag=None):
                dve.wait_ge(mt_full, b * 4 + (g + 1))
                if flag is not None:
                    dve.tensor_scalar(all_kept[0:1, flag:flag + 1], misc[bank_of(f"max_t{g}")][0:1, NQ:NQ + 1], 0.0, None,
                                      ALU.is_equal).then_inc(flag_ok, 1)
                if g % 2 == 0:
                    dve.wait_ge(qs_ok, b * 2 + (g // 2 + 1))
                if not (isinstance(b, int) and b == 0 and g < 2):
                    dve.wait_ge(st_full, b * 32 + (g * 8 - 8))
                dve.tensor_tensor(q_shift[:, g % 2, :], misc[bank_of(f"max_t{g}")][:, 0:NQ], q_stack[:, p, g, :].bitcast(F32),
                                  ALU.add).then_inc(qshift_ok, 1)

            def normalise(b, p, q):
                heads = misc[bank_of(f"heads_t{q}")].rearrange("p (h r) -> p h r", r=R)
                dve.wait_ge(ht_full, b * 2 + (q + 1))
                dve.reciprocal(inv[:, q, :], heads[:, :, D]).then_inc(norm_step, 1)
                dve.wait_ge(norm_step, b * 2 + (q + 1))
                dve.tensor_tensor(attn[:, q, :].rearrange("p (h d) -> p h d", d=D), heads[:, :, 0:D],
                                  inv[:, q, :].unsqueeze(2).to_broadcast([P, H, D]), ALU.mult).then_inc(attn_ok, 1)

            def residual(b, p):
                dve.wait_ge(wo_full, b + 1)
                dve.wait_ge(xbo_ok, b + 1)
                dve.scalar_tensor_tensor(out=x1[:, :, :].rearrange("p t f -> p (t f)"), in0=misc[bank_of("wo")][:, 0:QT * E],
                                         scalar=tgates[:, 0:1], in1=x_bo[:, :, :].rearrange("p t f -> p (t f)"),
                                         op0=ALU.mult, op1=ALU.add).then_inc(x1_ok, 1)

            def logits_out(b):
                dve.wait_ge(lg_full, b + 1)
                dve.tensor_tensor(logits[:, bass.ds(b * QT, QT), :],
                                  misc[bank_of("logits")][:, 0:QT * NEXP].rearrange("p (t e) -> p t e", e=NEXP),
                                  rb_row.unsqueeze(1).to_broadcast([P, QT, NEXP]), ALU.add).then_inc(lg_ok, 1)

            def slots(b, p, before=None, after=None):
                for g in range(G):
                    last = g == G - 1 and not after
                    for j in range(8):
                        at_b, at_p, at_g, k, over = scores_at(b, p, g, j)
                        if not over or after:
                            row_max(at_b, at_p, at_g, k)
                            if k == 7:
                                minus_max(at_b, at_p, at_g)
                        if g == 3 and j == 5 and before:
                            logits_out(b - 1)
                        if j == 5 and not last:
                            if g < G - 1:
                                shift(b, p, g + 1, 1 - p if g == 2 and after else None)
                            else:
                                shift(b + 1, 1 - p, 0)
                        step = g * 8 + j
                        if after:
                            if step == 0:
                                ln_x(b + 1)
                            if step == 2:
                                k_lo_half(b + 1)
                            if step == 10:
                                q_lo_half(b + 1)
                        if before:
                            if step == 6:
                                normalise(b - 1, 1 - p, 0)
                            if step == 9:
                                normalise(b - 1, 1 - p, 1)
                            if step == 16:
                                residual(b - 1, 1 - p)
                        if 17 <= step <= 24:
                            steps = {17: [0], 18: [1, 2], 19: [3, 4], 20: [5, 6], 21: [7, 8], 22: [9, 10], 23: [11],
                                     24: [12]}[step]
                            if before:
                                ln_x1_statistics(b - 1, *steps)
                            else:
                                ln_x_statistics(slice(2 * QT, TT), 4 * QT + 11, *steps)
                        if before:
                            if step == 24:
                                ln_x1(b - 1)

            dve.memset(zero[:, :], 0.0).then_inc(zeroed_v, 1)
            dve.memset(v_one[:, 0, :, :, :], 0.0).then_inc(zeroed_v, 1)
            dve.wait_ge(zeroed_v, 2)
            dve.memset(v_one[:, 0, :, :, D:D + 1].rearrange("p t h r -> p (t h) r"), 1.0).then_inc(zeroed_v, 1)
            dve.wait_ge(ld_x0, 16)
            ln_x_statistics(slice(0, 2 * QT), 0, *range(13))
            ln_x(0)
            dve.wait_ge(ld_cols, 16)
            k_lo_half(0)
            dve.wait_ge(ld_sel, 16)
            dve.tensor_copy(sel[:, :, :, :].rearrange("p m g r -> p (m g r)"), selraw).then_inc(sel_ok, 1)
            dve.tensor_copy(attn[:, 0, :], cols[:, 3:4].to_broadcast([P, P])).then_inc(bvo_ok, 1)
            dve.memset(minus_masked[:, :], -MASKED).then_inc(zeroed_v, 1)
            dve.memset(ones[:, :], 1.0).then_inc(zeroed_v, 1)
            dve.memset(neg_m[:, :, :, :], 0.0).then_inc(zeroed_v, 1)
            dve.wait_ge(ld_ident, 16)
            dve.tensor_copy(ident_b[:, :], ident[:, :]).then_inc(ident_ok, 1)
            q_lo_half(0)
            dve.wait_ge(bvo_full, 1)
            dve.wait_ge(ld_rows, 16)
            dve.tensor_tensor(tg_bo[:, :], banks[:, 5, 0:E], rows[:, 0:E], ALU.add).then_inc(bvo_ok, 1)
            dve.wait_ge(bvo_ok, 2)
            dve.wait_ge(tanh_ok, 1)
            dve.tensor_scalar(tg_bo[:, :], tg_bo[:, :], tgates[:, 0:1], None, ALU.mult).then_inc(tgbo_ok, 1)
            for k in range(8):
                row_max(0, 0, 0, k)
            minus_max(0, 0, 0)
            row_max(0, 0, 1, 0)
            shift(0, 0, 0, 0)
            for k in range(1, EARLY - 8):
                row_max(0, 0, 1, k)
            dve.wait_ge(ld_x, 16)
            slots(0, 0, before=False, after=True)
            with dve.Fori(1, B - 2, 2) as i:
                slots(i, 1, before=True, after=True)
                slots(i + 1, 0, before=True, after=True)
            slots(B - 1, 1, before=True, after=False)
            normalise(B - 1, 1, 0)
            normalise(B - 1, 1, 1)
            residual(B - 1, 1)
            ln_x1_statistics(B - 1, *range(13))
            ln_x1(B - 1)
            logits_out(B - 1)

            count = [0]

            def step(ins):
                count[0] += 1
                ins.then_inc(rt_step, 1)
                dve.wait_ge(rt_step, count[0])

            def bc(a):
                return a.unsqueeze(2).to_broadcast([P, TT, NEXP])

            z, ez, pr, tmp = (rt[:, k, :, :] for k in range(4))
            low, total, above, _ = (rs[:, k, :] for k in range(4))
            dve.wait_ge(lg_ok, B)
            step(dve.tensor_reduce(low, logits[:, :, :], AX_X, ALU.max))
            dve.tensor_tensor(z, logits[:, :, :], bc(low), ALU.subtract).then_inc(z_ok, 1)
            dve.wait_ge(rexp_ok, 1)
            step(dve.tensor_reduce(total, ez, AX_X, ALU.add))
            step(dve.reciprocal(total, total))
            step(dve.tensor_tensor(pr, ez, bc(total), ALU.mult))
            for n in range(TT):
                step(dve.max(top8[:, n, :], rt[:, 2, n, :])) if n == TT - 1 else dve.max(top8[:, n, :], rt[:, 2, n, :])
            fourth = bc(top8[:, :, TOPK - 1])
            step(dve.tensor_tensor(z, pr, fourth, ALU.is_gt))
            step(dve.tensor_reduce(above, z, AX_X, ALU.add))
            step(dve.tensor_tensor(ez, pr, fourth, ALU.is_equal))
            flat = [rt[:, k, :, :].rearrange("p t e -> p (t e)") for k in range(4)]
            dve.wait_ge(ld_c, 48)
            step(dve.tensor_tensor_scan(flat[3], notfirst[:, :], flat[1], 0.0, ALU.mult, ALU.add))
            step(dve.tensor_tensor(tmp, tmp, bc(above), ALU.add))
            step(dve.scalar_tensor_tensor(out=flat[3], in0=flat[3], scalar=float(TOPK), in1=flat[1], op0=ALU.is_le, op1=ALU.mult))
            step(dve.tensor_tensor(z, z, tmp, ALU.add))
            step(dve.tensor_tensor(z, z, pr, ALU.mult))
            step(dve.tensor_reduce(total, z, AX_X, ALU.add))
            step(dve.reciprocal(total, total))
            dve.tensor_tensor(ez, z, bc(total), ALU.mult).then_inc(cw_ok, 1)
            for c in range(4):
                dve.wait_ge(cwt_full, c + 1)
                dve.tensor_copy(cw_t[:, c * CH:(c + 1) * CH], acc[c][0:NEXP, :]).then_inc(cwt_ok, 1)

            def weigh(e, k, p):
                v = e * UNITS_E + k
                half = k % 2
                dve.wait_ge(gelu_ok, v + 1)
                if k == 0:
                    dve.wait_ge(ld_cw[p], e * 8 + (16 if p == 0 else 8))
                if not (isinstance(e, int) and e == 0 and k < 2):
                    dve.wait_ge(g_hi_ok, v - 1)
                    dve.wait_ge(g_lo_ok, v - 1)
                dve.tensor_tensor(gw[k % 2], gel[k % 2], cw[p][:, half * HALF:(half + 1) * HALF], ALU.mult).then_inc(gw_ok, 1)

            def lo_half(v, par):
                dve.wait_ge(g_hi_ok, v + 1)
                dve.tensor_tensor(g_lo[par], gw[par], g_hi[par].bitcast(F32), ALU.subtract).then_inc(g_lo_ok, 1)

            def expert(e, p, first=False):
                for k in range(UNITS_E):
                    weigh(e, k, p)
                    if not (first and k == 0):
                        lo_half(e * UNITS_E + (k - 1), (k - 1) % 2)

            expert(0, 0, first=True)
            expert(1, 1)
            with dve.Fori(2, NEXP - 1, 2) as i:
                expert(i, 0)
                expert(i + 1, 1)
            lo_half(NEXP * UNITS_E - 1, 1)
            dve.wait_ge(ff_done, NEXP * UNITS_E)
            for c in range(4):
                cols_c = x1_t[:, c * CH:(c + 1) * CH]
                dve.scalar_tensor_tensor(out=cols_c, in0=acc[c], scalar=tgates[:, 1:2], in1=cols_c, op0=ALU.mult,
                                         op1=ALU.add).then_inc(out_ok, 1)

        @block.tensor
        def _(pe):
            def taken(task, b):
                if task.startswith("max_t"):
                    return qshift_ok, b * 4 + (int(task[-1]) + 1)
                if task.startswith("heads_t"):
                    return attn_ok, b * 2 + (int(task[-1]) + 1)
                if task.startswith("q_stack"):
                    return qs_ok, b * 2 + (int(task[-1]) + 1)
                if task.startswith("k_stack"):
                    return ks_ok, b * 4 + (int(task[-1]) + 1)
                return {"xn_t": xnt_ok, "attn_t": attnt_ok, "q": qlo_ok, "k": klo_ok, "v": v_ok, "wo": x1_ok,
                        "x1_t": x1t_ok, "logits": lg_ok}[task], b + 1

            def misc_bank(task, b):
                if task == "v" and not isinstance(b, int):
                    return misc[bank_of(task)]
                for n in range(MISC_AT[task] - 1, -2 * len(MISC), -1):
                    before, other, bank = MISC[n % len(MISC)]
                    at = b + (n // len(MISC) + other)
                    if bank == bank_of(task) and (not isinstance(at, int) or 0 <= at < B):
                        pe.wait_ge(*taken(before, at))
                        break
                return misc[bank_of(task)]

            def transpose_xn(b):
                bank = misc_bank("xn_t", b)
                pe.wait_ge(ln_done[0], b * 2 + 4)
                for q in range(QT):
                    last = pe.transpose(bank[:, q * P:(q + 1) * P], xn[:, q, :], ident[:, :])
                last.then_inc(xnt_full, 1)

            def project_q(b):
                bank = misc_bank("q", b)
                pe.wait_ge(xnt_ok, b + 2)
                pe.matmul(bank[:, 0:NQ], wqkvo[:, 0, :], xn_t[:, :], start=True, stop=True).then_inc(q_full, 1)

            def project_k(b, p):
                bank = misc_bank("k", b)
                pe.wait_ge(ld_ctx[p], ctx_count(b + 1, p))
                pe.matmul(bank, wqkvo[:, 1, :], ctx_t[:, p, :], start=True, stop=True).then_inc(k_full, 1)

            def project_v(b, p):
                bank = misc_bank("v", b)
                for kt in range(KT):
                    last = pe.matmul(bank[:, kt * E:(kt + 1) * E], ctx_t[:, p, kt * P:(kt + 1) * P], wqkvo[:, 2, :],
                                     start=True, stop=True)
                last.then_inc(v_full, 1)

            def stack_q(b, n):
                bank = misc_bank(f"q_stack{n}", b)
                pe.wait_ge(qlo_ok, b + 2)
                for s in range(2):
                    out, g = bank[:, s * NQ:(s + 1) * NQ], 2 * n + s
                    pe.matmul(out, sel[:, 0, g, :], q_hi[:, :], start=True, stop=False)
                    last = pe.matmul(out, sel[:, 1, g, :], q_lo[:, :], start=False, stop=True)
                last.then_inc(qs_full, 1)

            def stack_k(b, g):
                bank = misc_bank(f"k_stack{g}", b)
                pe.wait_ge(klo_ok, b + 2)
                pe.matmul(bank, sel[:, 2, g, :], k_hi[:, :], start=True, stop=False)
                pe.matmul(bank, sel[:, 3, g, :], k_lo[:, :], start=False, stop=True).then_inc(ks_full, 1)

            def transpose_heads(b, q):
                bank = misc_bank(f"heads_t{q}", b)
                pe.wait_ge(heads_out, b * 4)
                for g in range(G):
                    last = pe.transpose(bank[:, g * P:(g + 1) * P], out_g[:, g, q * P:(q + 1) * P], ident[:, :])
                last.then_inc(ht_full, 1)

            def transpose_attn(b):
                bank = misc_bank("attn_t", b)
                pe.wait_ge(attn_ok, b * 2)
                for q in range(QT):
                    last = pe.transpose(bank[:, q * P:(q + 1) * P], attn[:, q, :], ident[:, :])
                last.then_inc(at_full, 1)

            def project_o(b):
                bank = misc_bank("wo", b)
                pe.wait_ge(attnt_ok, b)
                for q in range(QT):
                    last = pe.matmul(bank[:, q * E:(q + 1) * E], attn_t[:, q * P:(q + 1) * P], wqkvo[:, 3, :],
                                     start=True, stop=True)
                last.then_inc(wo_full, 1)

            def transpose_x1(b):
                bank = misc_bank("x1_t", b)
                pe.wait_ge(ln_done[1], b * 2)
                for q in range(QT):
                    pe.transpose(bank[:, q * P:(q + 1) * P], xn2[:, q, :], ident[:, :])
                for q in range(QT):
                    last = pe.transpose(bank[:, NQ + q * P:NQ + (q + 1) * P], x1[:, q, :], ident[:, :])
                last.then_inc(x1t_full, 1)

            def route(b):
                bank = misc_bank("logits", b)
                pe.wait_ge(xn2t_ok, b)
                for q in range(QT):
                    last = pe.matmul(bank[:, q * NEXP:(q + 1) * NEXP], xn2_t[:, q * P:(q + 1) * P], rw[:, :],
                                     start=True, stop=True)
                last.then_inc(lg_full, 1)

            def transpose_max(b, g, flag=None):
                bank = misc_bank(f"max_t{(g + 1) % G}", b)
                pe.wait_ge(negm_ok, b * 4 + (g + 2))
                for q in range(QT):
                    last = pe.transpose(bank[:, q * P:(q + 1) * P], neg_m[:, (g + 1) % 2, q, :], ident[:, :])
                if flag is not None:
                    pe.wait_ge(maskt_ok, b + 2)
                    last = pe.matmul(bank[0:1, NQ:NQ + 1], mask_sum[:, flag:flag + 1], ones[:, :], start=True, stop=True)
                last.then_inc(mt_full, 1)

            def scores(b, p, g, k):
                qt, i = k // HG, k % HG
                if k == 0:
                    pe.wait_ge(pad_ok, b * 4 + (g + 1))
                    if g % 2 == 0:
                        pe.wait_ge(qs_ok, b * 2 + (g // 2 + 1))
                before = {0: -1, 1: 0, 2: -2}.get(k, k - SC + 1)
                wait(pe, max_done, b * 32 + (g * 8 + before))
                pe.matmul(sc[k % SC], q_stack[:, p, g, qt * P:(qt + 1) * P], k_pad[:, p, HG * g + i, :],
                          start=True, stop=True).then_inc(sc_full, 1)

            def scores_t(b, p, g, j, masked):
                kt, pair = j // 2, j % 2
                if j == 0:
                    pe.wait_ge(qshift_ok, b * 4 + (g + 1))
                    if g == 0:
                        pe.wait_ge(maskt_ok, b + 1)
                wait(pe, exp_done, b * 32 + (g * 8 + j - 1))
                if masked:
                    pe.matmul(st[j % 2], ident_b[:, :], maskt[:, p, kt, :].unsqueeze(1).to_broadcast([P, 2, NQ]),
                              start=True, stop=False)
                for s in range(2):
                    last = pe.matmul(st[j % 2][:, s * NQ:(s + 1) * NQ],
                                     k_pad[:, p, HG * g + 2 * pair + s, kt * P:(kt + 1) * P], q_shift[:, g % 2, :],
                                     start=not masked, stop=not masked or s == 1)
                last.then_inc(st_full, 1)

            def values(b, p, g, kt):
                if kt == 0:
                    if g == 0:
                        pe.wait_ge(v_ok, b + 1)
                    if isinstance(b, int) and b == 0 and g == 0:
                        pe.wait_ge(tgbo_ok, 1)
                    else:
                        pe.wait_ge(heads_out, b * 4 + g)
                pe.wait_ge(exp_done, b * 32 + (g * 8 + 2 * kt + 2))
                for i in range(HG):
                    last = pe.matmul(ov[R * i:R * (i + 1), :], v_one[:, p, kt, HG * g + i, :],
                                     probs[:, kt, i * NQ:(i + 1) * NQ], start=kt == 0, stop=kt == KT - 1)
                last.then_inc(pv_done, 1)

            def slots(b, p, before=None, after=None):
                wait_apart(pe, flag_ok, b + 1)
                kept = pe.value_load(all_kept[0:1, p:p + 1])
                with pe.If(kept > 0):
                    batch(b, p, before, after, masked=False)
                with pe.If(kept < 1):
                    batch(b, p, before, after, masked=True)

            def batch(b, p, before, after, masked):
                for g in range(G):
                    last = g == G - 1 and not after
                    for j in range(8):
                        if j == 5 and not last:
                            transpose_max(b, g, 1 - p if g == 2 and after else None)
                        scores_t(b, p, g, j, masked)
                        at_b, at_p, at_g, k, over = scores_at(b, p, g, j)
                        if not over or after:
                            scores(at_b, at_p, at_g, k)
                        if j == 1 and g:
                            values(b, p, g - 1, KT - 1)
                        if j == 1 and not g and before:
                            values(b - 1, 1 - p, G - 1, KT - 1)
                        if j in (3, 5, 7):
                            values(b, p, g, (j - 3) // 2)
                        step = g * 8 + j
                        if after:
                            if step == 0:
                                project_k(b, 1 - p)
                            if step == 1:
                                project_v(b, 1 - p)
                            if step == 3:
                                transpose_xn(b)
                            if step == 8:
                                project_q(b)
                        if before:
                            if step in (5, 8):
                                transpose_heads(b, (5, 8).index(step))
                            if step == 11:
                                transpose_attn(b)
                        if step == 13 and after:
                            stack_k(b, 0)
                        if step == 15 and before:
                            project_o(b)
                        if after:
                            if step in (16, 24):
                                stack_q(b, (16, 24).index(step))
                            if step == 18:
                                stack_k(b, 1)
                                stack_k(b, 2)
                            if step == 22:
                                stack_k(b, 3)
                        if before:
                            if step == 26:
                                transpose_x1(b)
                            if step == 28:
                                route(b)

            pe.wait_ge(ld_w, 16)
            project_k(-1, 0)
            project_v(-1, 0)
            pe.wait_ge(ld_ident, 16)
            transpose_xn(-1)
            project_q(-1)
            pe.wait_ge(sel_ok, 1)
            stack_k(-1, 0)
            stack_q(-1, 0)
            pe.wait_ge(bvo_ok, 1)
            pe.matmul(banks[:, 5, 0:E], attn[:, 0, :], wqkvo[:, 3, :], start=True, stop=True).then_inc(bvo_full, 1)
            stack_k(-1, 1)
            for k in range(3):
                scores(0, 0, 0, k)
            stack_k(-1, 2)
            for k in range(3, 8):
                scores(0, 0, 0, k)
            stack_k(-1, 3)
            scores(0, 0, 1, 0)
            stack_q(-1, 1)
            pe.wait_ge(zeroed_v, 6)
            transpose_max(-1, 3, 0)
            for k in range(1, EARLY - 8):
                scores(0, 0, 1, k)
            pe.wait_ge(ident_ok, 1)
            pe.wait_ge(zeroed_v1, 2)
            slots(0, 0, before=False, after=True)
            pe.wait_ge(ld_c, 48)
            with pe.Fori(1, B - 2, 2) as i:
                slots(i, 1, before=True, after=True)
                slots(i + 1, 0, before=True, after=True)
            slots(B - 1, 1, before=True, after=False)
            values(B - 1, 1, G - 1, KT - 1)
            transpose_heads(B, 0)
            transpose_heads(B, 1)
            transpose_attn(B)
            project_o(B)
            transpose_x1(B)
            route(B)

            def hidden(e, k, p):
                v = e * UNITS_E + k
                mt, half = k // 2, k % 2
                if k == 0:
                    pe.wait_ge(w_lo_ok, e + 1)
                if not (isinstance(e, int) and e == 0 and k < 2):
                    pe.wait_ge(gelu_ok, v - 1)
                w = slice(mt * P, (mt + 1) * P)
                for c in range(2):
                    h = slice(half * HALF + c * CH, half * HALF + (c + 1) * CH)
                    pe.matmul(hid[k % 2][:, c, :], w_hi[p][:, w], h_lo[:, h], start=True, stop=False)
                    pe.matmul(hid[k % 2][:, c, :], w_lo[p][:, w], h_hi[:, h], start=False, stop=False)
                    last = pe.matmul(hid[k % 2][:, c, :], w_hi[p][:, w], h_hi[:, h], start=False, stop=True)
                last.then_inc(hid_full, 1)

            def output(e, k, p):
                v = e * UNITS_E + k
                mt, half = k // 2, k % 2
                pe.wait_ge(g_lo_ok, v + 1)
                w = slice(FF + mt * E, FF + (mt + 1) * E)
                for c in range(2):
                    g, out = slice(c * CH, (c + 1) * CH), acc[2 * half + c]
                    for wt, gt in ((w_hi, g_lo), (w_lo, g_hi), (w_hi, g_hi)):
                        last = pe.matmul(out, wt[p][:, w], gt[k % 2][:, g], start=False, stop=True, skip_group_check=True)
                last.then_inc(ff_done, 1)

            def expert(e, p, final=False):
                for k in range(UNITS_E):
                    if k + AHEAD < UNITS_E:
                        hidden(e, k + AHEAD, p)
                    elif not final:
                        hidden(e + 1, k + AHEAD - UNITS_E, 1 - p)
                    output(e, k, p)

            pe.wait_ge(hlo_ok, B)
            hidden(0, 0, 0)
            hidden(0, 1, 0)
            pe.wait_ge(cw_ok, 1)
            pe.wait_ge(x1t_ok, B)
            for c in range(4):
                for n in range(4):
                    last = pe.transpose(acc[c][0:NEXP, n * P:(n + 1) * P], rt[:, 1, 4 * c + n, :], ident[:, :])
                last.then_inc(cwt_full, 1)
            for c in range(4):
                pe.wait_ge(cwt_ok, c + 1)
                pe.matmul(acc[c], b2[:, :], cw_t[:, c * CH:(c + 1) * CH], start=True, stop=True)
            for k in range(2, AHEAD):
                hidden(0, k, 0)
            with pe.Fori(0, NEXP - 3, 2) as i:
                expert(i, 0)
                expert(i + 1, 1)
            expert(NEXP - 2, 0)
            expert(NEXP - 1, 1, final=True)


def kernel(x, ctx_1024, mask_BxSxS2_bf1, g_xattn, g_ffn, L0_xattn_Wq, L0_xattn_bq, L0_xattn_Wk, L0_xattn_bk,
           L0_xattn_Wv, L0_xattn_bv, L0_xattn_Wo, L0_xattn_bo, L0_ffn_router_w, L0_ffn_router_b, L0_ffn_w1,
           L0_ffn_b1, L0_ffn_w2, L0_ffn_b2):
    import concourse.bacc as bacc
    from concourse.bass_utils import run_bass_kernel_spmd

    def arr(a):
        return np.asarray(a)

    mask = arr(mask_BxSxS2_bf1).view(np.uint8)
    sel, ones = stack_selectors()
    notfirst = np.ones((TT, NEXP), np.float32)
    notfirst[:, 0] = 0.0
    w1 = arr(L0_ffn_w1)
    w2 = arr(L0_ffn_w2).reshape(NEXP, MT, P, E).transpose(0, 2, 1, 3).reshape(NEXP, P, MT * E)
    b1 = arr(L0_ffn_b1).reshape(NEXP, MT, P).transpose(0, 2, 1)
    arrays = {
        "x": arr(x).reshape(TOK, E),
        "ctx_t": arr(ctx_1024).transpose(0, 2, 1),
        "maskq": mask,
        "maskt": mask.transpose(0, 2, 1),
        "wqkvo": np.concatenate([arr(w).T for w in (L0_xattn_Wq, L0_xattn_Wk, L0_xattn_Wv, L0_xattn_Wo)], axis=1),
        "cols": np.stack([arr(L0_xattn_bq), arr(L0_xattn_bk), ones[:, 0], arr(L0_xattn_bv)], axis=1),
        "rows": np.concatenate([arr(a).reshape(1, -1) for a in (L0_xattn_bo, L0_ffn_router_b, g_xattn,
                                                                 g_ffn)], axis=1),
        "ident": np.eye(P, dtype=np.float32),
        "sel": sel,
        "notfirst": notfirst.reshape(1, -1),
        "router_w": arr(L0_ffn_router_w),
        "b2": arr(L0_ffn_b2),
        "experts": np.concatenate([w1, w2, b1], axis=2),
    }
    arrays = {k: np.ascontiguousarray(a) for k, a in arrays.items()}
    nc = bacc.Bacc("TRN2", target_bir_lowering=False, num_devices=1)
    tensors = {k: nc.dram_tensor("in_" + k, a.shape, mybir.dt.from_np(a.dtype), kind="ExternalInput").ap()
               for k, a in arrays.items()}
    tensors["cw"] = nc.dram_tensor("expert_weights", (NEXP, TOK), F32, kind="Internal").ap()
    tensors["out"] = nc.dram_tensor("out", (E, TOK), F32, kind="ExternalOutput").ap()
    build(nc, tensors)
    r = run_bass_kernel_spmd(nc, [{"in_" + k: a for k, a in arrays.items()}], core_ids=[0])
    return np.ascontiguousarray(r.results[0]["out"].T).reshape(B, NQ, E)
```

```python
from contextlib import ExitStack

import numpy as np

import concourse.bass as bass
from concourse import mybir

F32 = mybir.dt.float32
F32R = mybir.dt.float32r
BF16 = mybir.dt.bfloat16
I32 = mybir.dt.int32
ALU = mybir.AluOpType
ACT = mybir.ActivationFunctionType
AX_X = mybir.AxisListType.X

B, NQ, NK, E = 8, 256, 512, 128
H, D = 16, 8
P = 128
QT, KT = NQ // P, NK // P
G, HG = 4, 4
R = 32
NEXP, TOPK, FF = 16, 4, 256
MT = FF // P
TOK = B * NQ
TT = TOK // P
CH = 512
SC = 3
EARLY = 13
UNITS_E = MT * 2
EARLY_E = 4
FIRST = [(e, 2 * half + mt) for half in range(2) for e in range(EARLY_E) for mt in range(MT)]
POOLS = 4
AHEAD = 3
SCALE = float(D) ** -0.5
EPS = 1e-5
MASKED = 1e30
LN_STEPS = 2 * QT + 2 + 9
GUESS = float(0x5F3759DF - 2 ** 30 - 2 ** 22)


def stack_selectors():
    sel = np.zeros((P, 4, G, P), np.float32)
    for g in range(G):
        for i in range(HG):
            for d in range(D):
                f, r = (g * HG + i) * D + d, i * R + 2 + d
                for matrix, block in ((0, 0), (0, 1), (1, 2), (2, 0), (3, 1), (2, 2)):
                    sel[f, matrix, g, r + block * D] = 1.0
    ones = np.zeros((P, 1), np.float32)
    for i in range(HG):
        ones[i * R:i * R + 2] = 1.0
    return sel.reshape(P, 4 * G * P), ones


def build(nc, t):
    ctx = ExitStack()
    with ctx:
        def sb(name, shape, dt=F32):
            return ctx.enter_context(nc.sbuf_tensor(name, shape, dt))

        def sem(name):
            return ctx.enter_context(nc.semaphore(name))

        wqkvo = sb("wqkvo", [P, 4, E])
        cols = sb("cols", [P, 4])
        rows = sb("rows", [P, E + NEXP + 2])
        rb_row = rows[:, E:E + NEXP]
        gates = rows[:, E + NEXP:]
        ident = sb("ident", [P, P])
        ident_b = sb("ident_b", [P, P], BF16)
        sel = sb("sel", [P, 4, G, P], F32R)
        notfirst = sb("notfirst", [P, TT * NEXP])
        rw = sb("rw", [P, NEXP])
        b2 = sb("b2", [NEXP, E])
        tgates = sb("tgates", [P, 2])
        tg_bo = sb("tg_bo", [P, E])

        x_sb = sb("x_sb", [P, TT, E])
        ctx_t = sb("ctx_t", [P, 2, NK])
        xn = sb("xn", [P, QT, E])
        xn_t = sb("xn_t", [P, NQ])
        q_hi, q_lo = sb("q_hi", [P, NQ], F32R), sb("q_lo", [P, NQ], F32R)
        k_hi, k_lo = sb("k_hi", [P, NK], F32R), sb("k_lo", [P, NK], F32R)
        k_stack = sb("k_stack", [P, 2, NK])
        k_pad = sb("k_pad", [P, 2, H, NK], F32R)
        q_stack = sb("q_stack", [P, 2, G, NQ], F32R)
        q_shift = sb("q_shift", [P, 2, NQ], F32R)
        v_one = sb("v_one", [P, 2, KT, H, R])
        probs = sb("probs", [P, KT, HG * NQ])
        selraw = probs[:, 0:2, :].rearrange("p t n -> p (t n)")
        maskq_u8 = sb("maskq_u8", [P, QT, NK], mybir.dt.uint8)
        maskt_u8 = sb("maskt_u8", [P, KT, NQ], mybir.dt.uint8)
        maskq = sb("maskq", [P, 2, QT, NK], BF16)
        maskt = sb("maskt", [P, 2, KT, NQ], BF16)
        mask_sum = sb("mask_sum", [P, 2])
        all_kept = sb("all_kept", [1, 2], I32)
        minus_masked = sb("minus_masked", [P, 1])
        ones, zero = sb("ones", [P, 1]), sb("zero", [P, 1])
        maxes = sb("maxes", [P, 2, QT, H])
        neg_m = sb("neg_m", [P, 2, QT, P])
        out_g = sb("out_g", [P, G, NQ])
        dead = sb("dead", [P, 3, QT])
        inv = sb("inv", [P, 2, H])
        attn = sb("attn", [P, QT, E])
        attn_t = sb("attn_t", [P, NQ])
        x_bo = sb("x_bo", [P, QT, E])
        x1 = sb("x1", [P, QT, E])
        xn2 = sb("xn2", [P, QT, E])
        xn2_t = sb("xn2_t", [P, NQ])
        stats = sb("stats", [P, 2, TT, 6])
        meanvar = sb("meanvar", [P, 2, TT, 2])
        rstd = sb("rstd", [P, 2, 3, TT])
        x1_t = sb("x1_t", [P, TOK])
        h_hi, h_lo = sb("h_hi", [P, TOK], F32R), sb("h_lo", [P, TOK], F32R)
        logits = sb("logits", [P, TT, NEXP])
        top8 = sb("top8", [P, TT, 8])
        rt = sb("rt", [P, 4, TT, NEXP])
        rs = sb("rs", [P, 4, TT])
        cw_t = x_sb[0:NEXP, :, :].rearrange("p t f -> p (t f)")

        banks = ctx.enter_context(nc.psum_tensor("banks", [P, 8, CH], F32))
        sc = [banks[:, n, :] for n in range(SC)]
        st = [banks[:, 3, :], banks[:, 4, :]]
        ov = banks[:, 5, 0:NQ]
        misc = [banks[:, 6, :], banks[:, 7, :]]
        hid = [banks[:, 0:2, :], banks[:, 2:4, :]]
        acc = [banks[:, 4 + c, :] for c in range(4)]

        MISC = [("k", 1, 0), ("v", 1, 1), ("xn_t", 1, 1), ("max_t1", 0, 0), ("heads_t0", -1, 1), ("q", 1, 0),
                ("heads_t1", -1, 1), ("attn_t", -1, 1), ("max_t2", 0, 0), ("k_stack0", 1, 1), ("wo", -1, 1),
                ("q_stack0", 1, 0), ("k_stack1", 1, 0), ("k_stack2", 1, 1), ("max_t3", 0, 0), ("k_stack3", 1, 1),
                ("q_stack1", 1, 0), ("x1_t", -1, 1), ("logits", -1, 1), ("max_t0", 1, 0)]
        MISC_AT = {task: n for n, (task, _, _) in enumerate(MISC)}

        def scores_at(b, p, g, j):
            over, n = divmod(g * 8 + j + EARLY, G * 8)
            return b + over, (p + over) % 2, n // 8, n % 8, over

        def bank_of(task):
            return MISC[MISC_AT[task]][2]

        ld_x0, ld_x, ld_w, ld_cols, ld_rows, ld_ident, ld_c, ld_sel = (sem(n) for n in (
            "ld_x0", "ld_x", "ld_w", "ld_cols", "ld_rows", "ld_ident", "ld_c", "ld_sel"))
        ld_ctx = [sem("ld_ctx0"), sem("ld_ctx1")]
        ld_mask = sem("ld_mask")
        ld_exp = [sem("ld_exp0"), sem("ld_exp1")]
        st_cw, st_out = sem("st_cw"), sem("st_out")
        ld_cw = [sem("ld_cw0"), sem("ld_cw1")]
        ld_first = [sem(f"ld_first{e}") for e in range(EARLY_E)]
        ident_ok, zeroed_v, zeroed_v1, sel_ok, tanh_ok, bvo_full, bvo_ok, tgbo_ok = (sem(n) for n in (
            "ident_ok", "zeroed_v", "zeroed_v1", "sel_ok", "tanh_ok", "bvo_full", "bvo_ok", "tgbo_ok"))
        zeroed = [sem("zeroed0"), sem("zeroed1")]
        xnt_full, q_full, k_full, v_full, qs_full, ks_full, mt_full, ht_full, at_full, wo_full, x1t_full, lg_full = (
            sem(n + "_full") for n in ("xnt", "q", "k", "v", "qs", "ks", "mt", "ht", "at", "wo", "x1t", "lg"))
        sc_full, max_done, st_full, exp_done, pv_done, heads_out = (sem(n) for n in (
            "sc_full", "max_done", "st_full", "exp_done", "pv_done", "heads_out"))
        ln_done = [sem("ln1_done"), sem("ln2_done")]
        ln_step = [sem("ln1_step"), sem("ln2_step")]
        xnt_ok, qhi_ok, qlo_ok, khi_ok, klo_ok, v_ok, qs_ok, ks_ok, pad_ok, maskq_ok, maskt_ok, flag_ok = (sem(n) for n in (
            "xnt_ok", "qhi_ok", "qlo_ok", "khi_ok", "klo_ok", "v_ok", "qs_ok", "ks_ok", "pad_ok", "maskq_ok", "maskt_ok",
            "flag_ok"))
        negm_hi, negm_ok, qshift_ok, norm_step, attn_ok, attnt_ok = (sem(n) for n in (
            "negm_hi", "negm_ok", "qshift_ok", "norm_step", "attn_ok", "attnt_ok"))
        xbo_step, xbo_ok, x1_ok, xn2t_ok, x1t_ok, hhi_ok, hlo_ok, lg_ok = (sem(n) for n in (
            "xbo_step", "xbo_ok", "x1_ok", "xn2t_ok", "x1t_ok", "hhi_ok", "hlo_ok", "lg_ok"))
        rt_step, z_ok, rexp_ok, cw_ok, cwt_full, cwt_ok = (sem(n) for n in (
            "rt_step", "z_ok", "rexp_ok", "cw_ok", "cwt_full", "cwt_ok"))
        w_hi_ok, w_lo_ok, hid_full, gelu_ok, gw_ok, g_hi_ok, g_lo_ok, ff_done, out_ok = (sem(n) for n in (
            "w_hi_ok", "w_lo_ok", "hid_full", "gelu_ok", "gw_ok", "g_hi_ok", "g_lo_ok", "ff_done", "out_ok"))

        WCOLS = FF + MT * E
        HALF = 2 * CH
        w_raw = sb("w_raw", [P, 2, WCOLS])
        b1 = sb("b1", [P, NEXP, MT])
        under = k_pad[:, 0, :, :].rearrange("p h n -> p (h n)")
        under1 = k_pad[:, 1, :, :].rearrange("p h n -> p (h n)")
        w_halves = [[(u[:, n * WCOLS:(n + 1) * WCOLS], u[:, (2 + n) * WCOLS:(3 + n) * WCOLS]) for n in (0, 1)]
                    for u in (under, under1)]

        def halves_of(e, p):
            return w_halves[1 if isinstance(e, int) and 2 <= e < EARLY_E else 0][p]

        g_hi = [under[:, n * HALF:(n + 1) * HALF] for n in (2, 3)]
        g_lo = [under[:, n * HALF:(n + 1) * HALF] for n in (4, 5)]
        gel = [probs[:, n, :] for n in (0, 1)]
        gw = [probs[:, n, :] for n in (2, 3)]
        under = v_one[:, :, :, :, :].rearrange("p a t h r -> p (a t h r)")
        cw = [under[:, n * TOK:(n + 1) * TOK] for n in (0, 1)]
        cw_first = [under[:, n * HALF:(n + 1) * HALF] for n in range(EARLY_E)]

        block = ctx.enter_context(nc.Block())

        def last_unit(e):
            return 1 + max(v for v, (expert, _) in enumerate(FIRST) if expert == e)

        def wait(eng, s, n):
            if not (isinstance(n, int) and n <= 0):
                eng.wait_ge(s, n)

        def wait_apart(eng, s, n):
            n = n if isinstance(n, int) else eng.to_reg(n)
            eng.wait_ge(ld_x0, 16)
            eng.wait_ge(s, n)

        def ctx_count(b, p):
            return b * 8 + (16 if p == 0 else 8)

        @block.sync
        def _(sp):
            sp.dma_start(wqkvo[:, :, :], t["wqkvo"].rearrange("p (m f) -> p m f", m=4)).then_inc(ld_w, 16)
            sp.dma_start(ctx_t[:, 0, :], t["ctx_t"][0]).then_inc(ld_ctx[0], 16)
            sp.dma_start(selraw, t["sel"]).then_inc(ld_sel, 16)
            sp.dma_start(maskq_u8[:, :, :], t["maskq"][0].rearrange("(t p) k -> p t k", p=P)).then_inc(ld_mask, 16)
            sp.dma_start(maskt_u8[:, :, :], t["maskt"][0].rearrange("(t p) q -> p t q", p=P)).then_inc(ld_mask, 16)
            sp.dma_start(x_sb[:, 2 * QT:, :], t["x"][2 * NQ:, :].rearrange("(t p) f -> p t f", p=P)).then_inc(ld_x, 16)
            sp.dma_start(ctx_t[:, 1, :], t["ctx_t"][1]).then_inc(ld_ctx[1], 16)
            sp.dma_start(notfirst[:, :], t["notfirst"].partition_broadcast(P)).then_inc(ld_c, 16)
            sp.dma_start(rw[:, :], t["router_w"]).then_inc(ld_c, 16)
            sp.dma_start(b2[:, :], t["b2"]).then_inc(ld_c, 16)
            sp.dma_start(b1[:, :, :], t["b1"]).then_inc(ld_c, 16)
            for e in range(2):
                sp.dma_start(w_raw[:, e, :], t["experts"][e]).then_inc(ld_exp[e], 16)

            def masks(b):
                wait_apart(sp, maskq_ok, b)
                wait_apart(sp, maskt_ok, b)
                sp.dma_start(maskq_u8[:, :, :], t["maskq"][b].rearrange("(t p) k -> p t k", p=P)).then_inc(ld_mask, 16)
                sp.dma_start(maskt_u8[:, :, :], t["maskt"][b].rearrange("(t p) q -> p t q", p=P)).then_inc(ld_mask, 16)

            masks(1)
            with sp.Fori(0, B - 3, 2) as i:
                for p in range(2):
                    b = i + p
                    wait_apart(sp, v_full, b + 1)
                    sp.dma_start(ctx_t[:, p, :], t["ctx_t"][b + 2]).then_inc(ld_ctx[p], 16)
                    masks(b + 2)
            def next_weights(e, p):
                wait_apart(sp, w_lo_ok, e + 1)
                sp.dma_start(w_raw[:, p, :], t["experts"][e + 2]).then_inc(ld_exp[p], 16)

            def next_cw(e, p, used):
                wait_apart(sp, gw_ok, used)
                sp.dma_start(cw[p], t["cw"][bass.ds(e + 2, 1), :].partition_broadcast(P)).then_inc(ld_cw[p], 16)

            next_weights(0, 0)
            next_weights(1, 1)
            for n in range(2):
                if n:
                    next_weights(2, 0)
                    next_weights(3, 1)
                sp.wait_ge(cwt_ok, 2 * n + 2)
                sp.dma_start(t["cw"][:, n * HALF:(n + 1) * HALF], cw_t[:, n * HALF:(n + 1) * HALF]).then_inc(st_cw, 16)
                sp.wait_ge(st_cw, 16 * n + 16)
                for e in range(EARLY_E):
                    if n:
                        sp.wait_ge(ld_first[e], 16)
                        sp.wait_ge(gw_ok, (e + 1) * MT)
                    sp.dma_start(cw_first[e], t["cw"][e:e + 1, n * HALF:(n + 1) * HALF].partition_broadcast(P)).then_inc(
                        ld_first[e], 16)
            next_cw(2, 0, last_unit(1))
            next_cw(3, 1, last_unit(3))
            with sp.Fori(EARLY_E, NEXP - 3, 2) as i:
                for p in range(2):
                    next_weights(i + p, p)
                    next_cw(i + p, p, (i + p) * UNITS_E + UNITS_E)
            for c in range(4):
                sp.wait_ge(out_ok, c + 1)
                sp.dma_start(t["out"][:, c * CH:(c + 1) * CH], x1_t[:, c * CH:(c + 1) * CH]).then_inc(st_out, 16)
            sp.wait_ge(st_out, 4 * 16)

        @block.gpsimd
        def _(pool):
            def mask_bias(b, p):
                wait_apart(pool, ld_mask, b * 32 + 32)
                if not isinstance(b, int) or b >= 2:
                    wait_apart(pool, max_done, b * 32 - 32)
                pool.tensor_scalar(maskq[:, p, :, :], maskq_u8[:, :, :], -1.0, MASKED, ALU.add, ALU.mult).then_inc(maskq_ok, 1)

            def x_plus_bo(b, p):
                if isinstance(b, int) and b == 0:
                    pool.wait_ge(tgbo_ok, 1)
                bo = tg_bo[:, :].unsqueeze(1).to_broadcast([P, QT, E])
                pool.tensor_tensor(x_bo[:, :, :], x_sb[:, bass.ds(b * QT, QT), :], bo, ALU.add).then_inc(xbo_step, 1)
                m = maxes[:, p, :, 0]
                wait_apart(pool, max_done, b * 32 + 8)
                pool.tensor_scalar(dead[:, 0, :], m, -1.0, -MASKED / 2, ALU.mult, ALU.add).then_inc(xbo_step, 1)
                wait_apart(pool, xbo_step, b * 4 + 2)
                pool.tensor_scalar(dead[:, 1, :], dead[:, 0, :], 0.0, MASKED, ALU.max, ALU.mult).then_inc(xbo_step, 1)
                wait_apart(pool, xbo_step, b * 4 + 3)
                pool.tensor_scalar(dead[:, 2, :], dead[:, 1, :], 0.0, None, ALU.mult).then_inc(xbo_step, 1)
                wait_apart(pool, xbo_step, b * 4 + 4)
                pool.tensor_tensor(x_bo[:, :, :], x_bo[:, :, :], dead[:, 2, :].unsqueeze(2).to_broadcast([P, QT, E]),
                                   ALU.add).then_inc(xbo_ok, 1)

            def h_halves(b):
                wait_apart(pool, xn2t_ok, b + 1)
                cols_b = bass.ds(b * NQ, NQ)
                pool.tensor_copy(h_hi[:, cols_b], xn2_t[:, :]).then_inc(hhi_ok, 1)
                wait_apart(pool, hhi_ok, b + 1)
                pool.tensor_tensor(h_lo[:, cols_b], xn2_t[:, :], h_hi[:, cols_b].bitcast(F32), ALU.subtract).then_inc(hlo_ok, 1)

            def pad(b, p, g):
                if g == 0:
                    pool.wait_ge(maskq_ok, b + 1)
                wait_apart(pool, ks_ok, b * G + g + 1)
                if isinstance(b, int) and b < 2:
                    pool.wait_ge(zeroed[p], g + 1)
                for i in range(HG):
                    last = pool.tensor_scalar(k_pad[R * i:R * (i + 1), p, HG * g + i, :], k_stack[R * i:R * (i + 1), g % 2, :],
                                              1.0, 0.0, ALU.mult, ALU.add)
                last.then_inc(pad_ok, 1)

            def batch(b, p):
                mask_bias(b, p)
                for g in range(G):
                    pad(b, p, g)
                wait_apart(pool, pad_ok, b * G + G)
                if not isinstance(b, int) or b >= 2:
                    h_halves(b - 2)
                x_plus_bo(b - 1, 1 - p)

            for g in range(G):
                pool.memset(k_pad[:, 0, HG * g:HG * (g + 1), :].bitcast(F32), 0.0).then_inc(zeroed[0], 1)
            pool.memset(v_one[:, 1, :, :, :], 0.0).then_inc(zeroed_v1, 1)
            pool.wait_ge(zeroed_v1, 1)
            pool.memset(v_one[:, 1, :, :, D:D + 1].rearrange("p t h r -> p (t h) r"), 1.0).then_inc(zeroed_v1, 1)
            mask_bias(0, 0)
            for g in range(G):
                pad(0, 0, g)
            pool.wait_ge(pad_ok, G)
            pool.wait_ge(ld_x, 16)
            batch(1, 1)
            with pool.Fori(2, B - 1, 2) as i:
                batch(i, 0)
                batch(i + 1, 1)

            def weight_halves(e, p):
                w_hi, w_lo = halves_of(e, p)
                wait_apart(pool, ld_exp[p], e * 8 + (16 if p == 0 else 8))
                if isinstance(e, int) and e < EARLY_E:
                    pool.wait_ge(exp_done, (B - 1) * 32 if e < 2 else B * 32)
                elif isinstance(e, int):
                    pool.wait_ge(ff_done, last_unit(e - EARLY_E))
                else:
                    wait_apart(pool, ff_done, e * UNITS_E - UNITS_E)
                pool.tensor_scalar(w_hi, w_raw[:, p, :], 1.0, 0.0, ALU.mult, ALU.add).then_inc(w_hi_ok, 1)
                pool.wait_ge(w_hi_ok, e + 1)
                pool.tensor_tensor(w_lo, w_raw[:, p, :], w_hi.bitcast(F32), ALU.subtract).then_inc(w_lo_ok, 1)

            pool.wait_ge(pad_ok, B * G)
            weight_halves(0, 0)
            weight_halves(1, 1)
            h_halves(B - 2)
            x_plus_bo(B - 1, 1)
            weight_halves(2, 0)
            weight_halves(3, 1)
            h_halves(B - 1)
            pool.wait_ge(g_lo_ok, 1)
            for v in range(1, POOLS):
                pool.wait_ge(g_hi_ok, v + 1)
                pool.tensor_tensor(g_lo[v % 2], gw[v % 2], g_hi[v % 2].bitcast(F32), ALU.subtract).then_inc(g_lo_ok, 1)
            weight_halves(4, 0)
            weight_halves(5, 1)
            with pool.Fori(6, NEXP - 1, 2) as i:
                weight_halves(i, 0)
                weight_halves(i + 1, 1)

        @block.scalar
        def _(act):
            def xn_t_copy(b):
                act.wait_ge(xnt_full, b + 1)
                act.activation(xn_t[:, :], misc[bank_of("xn_t")][:, 0:NQ], ACT.Copy).then_inc(xnt_ok, 1)

            def q_hi_half(b):
                act.wait_ge(q_full, b + 1)
                wait(act, qs_full, b * 2)
                act.activation(q_hi[:, :], misc[bank_of("q")][:, 0:NQ], ACT.Identity, bias=cols[:, 0:1]).then_inc(qhi_ok, 1)

            def k_hi_half(b):
                act.wait_ge(k_full, b + 1)
                wait(act, ks_full, b * G)
                act.activation(k_hi[:, :], misc[bank_of("k")], ACT.Identity, bias=cols[:, 1:2]).then_inc(khi_ok, 1)

            def q_stack_out(b, p, n):
                act.wait_ge(qs_full, b * 2 + n + 1)
                bank = bank_of(f"q_stack{n}")
                act.activation(q_stack[:, p, 2 * n:2 * n + 2, :].rearrange("p g q -> p (g q)"), misc[bank],
                               ACT.Copy).then_inc(qs_ok, 1)

            def k_stack_out(b, g):
                act.wait_ge(ks_full, b * G + g + 1)
                if not (isinstance(b, int) and b == 0 and g < 2):
                    act.wait_ge(pad_ok, b * G + g - 1)
                bank = bank_of(f"k_stack{g}")
                act.activation(k_stack[:, g % 2, :], misc[bank], ACT.Identity, bias=cols[:, 2:3]).then_inc(ks_ok, 1)

            def mask_bias_t(b, p):
                act.wait_ge(ld_mask, b * 32 + 32)
                act.activation(maskt[:, p, :, :].rearrange("p t q -> p (t q)"), maskt_u8[:, :, :].rearrange("p t q -> p (t q)"),
                               ACT.Identity, scale=MASKED, bias=minus_masked[:, :],
                               accum_out=mask_sum[:, p:p + 1]).then_inc(maskt_ok, 1)

            def v_out(b, p):
                act.wait_ge(v_full, b + 1)
                if not isinstance(b, int) or b >= 2:
                    act.wait_ge(pv_done, b * 16 - 16)
                act.activation(v_one[:, p, :, :, 0:D].rearrange("p t h d -> p (t h) d"),
                               misc[bank_of("v")].rearrange("p (h d) -> p h d", d=D), ACT.Copy).then_inc(v_ok, 1)

            def exp(b, g, j):
                kt, pair = j // 2, j % 2
                act.wait_ge(st_full, b * 32 + g * 8 + j + 1)
                if pair == 0:
                    wait(act, pv_done, b * 16 + g * 4 - 3 + kt)
                act.activation(probs[:, kt, pair * CH:(pair + 1) * CH], st[j % 2], ACT.Exp, scale=SCALE).then_inc(exp_done, 1)

            def heads_copy(b, g):
                act.wait_ge(pv_done, b * 16 + g * 4 + 4)
                act.activation(out_g[:, g, :], ov, ACT.Copy).then_inc(heads_out, 1)

            def attn_t_copy(b):
                act.wait_ge(at_full, b + 1)
                bank = bank_of("attn_t")
                act.activation(attn_t[:, :], misc[bank][:, 0:NQ], ACT.Copy).then_inc(attnt_ok, 1)

            def x1_t_copy(b):
                act.wait_ge(x1t_full, b + 1)
                bank = bank_of("x1_t")
                act.activation(xn2_t[:, :], misc[bank][:, 0:NQ], ACT.Copy).then_inc(xn2t_ok, 1)
                act.activation(x1_t[:, bass.ds(b * NQ, NQ)], misc[bank][:, NQ:], ACT.Copy).then_inc(x1t_ok, 1)

            def router_exp(n):
                act.wait_ge(z_ok, n + 1)
                half = slice(n * TT // 2, (n + 1) * TT // 2)
                act.activation(rt[:, 1, half, :], rt[:, 0, half, :], ACT.Exp).then_inc(rexp_ok, 1)

            def slots(b, p, before=None, after=None):
                for g in range(G):
                    for j in range(8):
                        exp(b, g, j)
                        if j == 1 and (before or g):
                            if g:
                                heads_copy(b, g - 1)
                            else:
                                heads_copy(b - 1, G - 1)
                        step = g * 8 + j
                        if after:
                            if step == 1:
                                k_hi_half(b + 1)
                            if step == 2:
                                v_out(b + 1, 1 - p)
                            if step == 4:
                                xn_t_copy(b + 1)
                            if step == 6:
                                mask_bias_t(b + 1, 1 - p)
                            if step == 9:
                                q_hi_half(b + 1)
                            if step in (14, 19, 20, 23):
                                k_stack_out(b + 1, (14, 19, 20, 23).index(step))
                            if step in (17, 25):
                                q_stack_out(b + 1, 1 - p, (17, 25).index(step))
                        if step == 25 and not after:
                            router_exp(0)
                        if before:
                            if step == 12:
                                attn_t_copy(b - 1)
                            if step == 27:
                                x1_t_copy(b - 1)

            act.dma_start(x_sb[:, 0:2 * QT, :], t["x"][0:2 * NQ, :].rearrange("(t p) f -> p t f", p=P)).then_inc(ld_x0, 16)
            act.dma_start(cols[:, :], t["cols"]).then_inc(ld_cols, 16)
            act.dma_start(ident[:, :], t["ident"]).then_inc(ld_ident, 16)
            act.dma_start(rows[:, :], t["rows"].partition_broadcast(P)).then_inc(ld_rows, 16)
            def zero_pad(g):
                act.activation(k_pad[:, 1, HG * g:HG * (g + 1), :].rearrange("p h n -> p (h n)"),
                               zero[:, :].to_broadcast([P, HG * NK]), ACT.Copy).then_inc(zeroed[1], 1)

            act.wait_ge(zeroed_v, 1)
            zero_pad(0)
            act.wait_ge(ld_cols, 16)
            k_hi_half(0)
            act.wait_ge(zeroed_v, 3)
            v_out(0, 0)
            xn_t_copy(0)
            q_hi_half(0)
            act.wait_ge(ld_rows, 16)
            act.activation(tgates[:, :], gates, ACT.Tanh).then_inc(tanh_ok, 1)
            k_stack_out(0, 0)
            q_stack_out(0, 0, 0)
            mask_bias_t(0, 0)
            for g in range(1, G):
                k_stack_out(0, g)
                if g == G - 1:
                    q_stack_out(0, 0, 1)
                zero_pad(g)
            act.wait_ge(zeroed_v1, 2)
            slots(0, 0, before=False, after=True)
            with act.Fori(1, B - 2, 2) as i:
                slots(i, 1, before=True, after=True)
                slots(i + 1, 0, before=True, after=True)
            slots(B - 1, 1, before=True, after=False)

            def gelu(v, k, e):
                wait_apart(act, hid_full, v + 1)
                if not isinstance(v, int):
                    wait_apart(act, gw_ok, v - 1)
                else:
                    wait(act, gw_ok, v - 1)
                mt = k % 2
                act.activation(gel[k % 2], hid[k % 2].rearrange("p a c -> p (a c)"), ACT.Gelu,
                               bias=b1[:, slice(e, e + 1) if isinstance(e, int) else bass.ds(e, 1), mt]).then_inc(gelu_ok, 1)

            def hi_half(v, par):
                act.wait_ge(gw_ok, v + 1)
                wait(act, ff_done, v - 1)
                act.activation(g_hi[par], gw[par], ACT.Copy).then_inc(g_hi_ok, 1)

            def first_gelu(v):
                gelu(v, FIRST[v][1], FIRST[v][0])

            def expert(e, p):
                for k in range(UNITS_E):
                    gelu(e * UNITS_E + k, k, e)
                    hi_half(e * UNITS_E + k - 1, (k - 1) % 2)

            heads_copy(B - 1, G - 1)
            attn_t_copy(B - 1)
            act.wait_ge(ld_c, 64)
            first_gelu(0)
            first_gelu(1)
            x1_t_copy(B - 1)
            hi_half(0, 0)
            first_gelu(2)
            hi_half(1, 1)
            router_exp(1)
            first_gelu(3)
            for v in range(4, len(FIRST)):
                hi_half(v - 2, v % 2)
                first_gelu(v)
            hi_half(len(FIRST) - 2, 0)
            with act.Fori(EARLY_E, NEXP - 1, 2) as i:
                expert(i, 0)
                expert(i + 1, 1)
            hi_half(NEXP * UNITS_E - 1, 1)

        @block.vector
        def _(dve):
            def statistics(n, base, src, at, step):
                half, y, tmp = (rstd[:, n, k, at] for k in range(3))
                if step == 0:
                    for q, tile in enumerate(src):
                        dve.bn_stats(stats[:, n, at.start + q, :], tile).then_inc(ln_step[n], 1)
                    return
                if step == 1:
                    wait_apart(dve, ln_step[n], base + len(src))
                    for q in range(len(src)):
                        dve.bn_aggr(meanvar[:, n, at.start + q, :], stats[:, n, at.start + q, :]).then_inc(ln_step[n], 1)
                    return
                dve.wait_ge(ln_step[n], base + (2 * len(src) + step - 2))
                if step == 2:
                    ins = dve.tensor_scalar(half, meanvar[:, n, at, 1], EPS, -0.5, ALU.add, ALU.mult)
                elif step == 3:
                    ins = dve.tensor_scalar(y.bitcast(I32), half.bitcast(I32), -0.5, GUESS, ALU.mult, ALU.add)
                elif step % 3 == 1:
                    ins = dve.tensor_tensor(tmp, y, y, ALU.mult)
                elif step % 3 == 2:
                    ins = dve.tensor_tensor(tmp, tmp, half, ALU.mult)
                else:
                    ins = dve.scalar_tensor_tensor(out=y, in0=tmp, scalar=1.5, in1=y, op0=ALU.add, op1=ALU.mult)
                ins.then_inc(ln_step[n], 1)

            def ln_x_statistics(tiles, count, *steps):
                for step in steps:
                    statistics(0, count, [x_sb[:, n, :] for n in range(tiles.start, tiles.stop)], tiles, step)
                if steps[-1] == 12:
                    dve.wait_ge(ln_step[0], count + 2 * (tiles.stop - tiles.start) + 11)

            def ln_x(b):
                for q in range(QT):
                    n = b * QT + q
                    n = slice(n, n + 1) if isinstance(n, int) else bass.ds(n, 1)
                    dve.tensor_scalar(xn[:, q, :], x_sb[:, n, :].rearrange("p t f -> p (t f)"), meanvar[:, 0, n, 0],
                                      rstd[:, 0, 1, n], ALU.subtract, ALU.mult).then_inc(ln_done[0], 1)

            def ln_x1_statistics(b, *steps):
                for step in steps:
                    if step == 0:
                        dve.wait_ge(x1_ok, b + 1)
                    statistics(1, b * LN_STEPS, [x1[:, q, :] for q in range(QT)], slice(0, QT), step)

            def ln_x1(b):
                dve.wait_ge(ln_step[1], b * LN_STEPS + LN_STEPS)
                for q in range(QT):
                    dve.tensor_scalar(xn2[:, q, :], x1[:, q, :], meanvar[:, 1, q, 0:1], rstd[:, 1, 1, q:q + 1],
                                      ALU.subtract, ALU.mult).then_inc(ln_done[1], 1)

            def q_lo_half(b):
                dve.wait_ge(qhi_ok, b + 1)
                dve.scalar_tensor_tensor(out=q_lo[:, :], in0=misc[bank_of("q")][:, 0:NQ], scalar=cols[:, 0:1],
                                         in1=q_hi[:, :].bitcast(F32), op0=ALU.add, op1=ALU.subtract).then_inc(qlo_ok, 1)

            def k_lo_half(b):
                dve.wait_ge(khi_ok, b + 1)
                dve.scalar_tensor_tensor(out=k_lo[:, :], in0=misc[bank_of("k")], scalar=cols[:, 1:2],
                                         in1=k_hi[:, :].bitcast(F32), op0=ALU.add, op1=ALU.subtract).then_inc(klo_ok, 1)

            def row_max(b, p, g, k):
                qt, i = k // HG, k % HG
                if g == 0 and k == 0:
                    dve.wait_ge(maskq_ok, b + 1)
                wait_apart(dve, sc_full, b * 32 + (g * 8 + k + 1))
                h = HG * g + i
                dve.tensor_tensor_reduce(sc[k % SC], sc[k % SC], maskq[:, p, qt, :], 1.0, -3.0e38, ALU.add, ALU.max,
                                         maxes[:, p, qt, h:h + 1]).then_inc(max_done, 1)

            def minus_max(b, p, g):
                dve.wait_ge(max_done, b * 32 + (g * 8 + 8))
                if not (isinstance(b, int) and b == 0 and g < 2):
                    dve.wait_ge(mt_full, b * 4 + (g - 1))
                m = maxes[:, p, :, HG * g:HG * (g + 1)]
                col = neg_m[:, g % 2, :, :].rearrange("p q (i r) -> p q i r", r=R)
                dve.tensor_scalar(col[:, :, :, 0].bitcast(F32R), m, -1.0, None, ALU.mult).then_inc(negm_hi, 1)
                dve.wait_ge(negm_hi, b * 4 + (g + 1))
                dve.scalar_tensor_tensor(out=col[:, :, :, 1], in0=m, scalar=-1.0, in1=col[:, :, :, 0], op0=ALU.mult,
                                         op1=ALU.subtract).then_inc(negm_ok, 1)

            def shift(b, p, g, flag=None):
                dve.wait_ge(mt_full, b * 4 + (g + 1))
                if flag is not None:
                    dve.tensor_scalar(all_kept[0:1, flag:flag + 1], misc[bank_of(f"max_t{g}")][0:1, NQ:NQ + 1], 0.0, None,
                                      ALU.is_equal).then_inc(flag_ok, 1)
                if g % 2 == 0:
                    dve.wait_ge(qs_ok, b * 2 + (g // 2 + 1))
                if not (isinstance(b, int) and b == 0 and g < 2):
                    dve.wait_ge(st_full, b * 32 + (g * 8 - 8))
                dve.tensor_tensor(q_shift[:, g % 2, :], misc[bank_of(f"max_t{g}")][:, 0:NQ], q_stack[:, p, g, :].bitcast(F32),
                                  ALU.add).then_inc(qshift_ok, 1)

            def normalise(b, p, q):
                heads = misc[bank_of(f"heads_t{q}")].rearrange("p (h r) -> p h r", r=R)
                dve.wait_ge(ht_full, b * 2 + (q + 1))
                dve.reciprocal(inv[:, q, :], heads[:, :, D]).then_inc(norm_step, 1)
                dve.wait_ge(norm_step, b * 2 + (q + 1))
                dve.tensor_tensor(attn[:, q, :].rearrange("p (h d) -> p h d", d=D), heads[:, :, 0:D],
                                  inv[:, q, :].unsqueeze(2).to_broadcast([P, H, D]), ALU.mult).then_inc(attn_ok, 1)

            def residual(b, p):
                dve.wait_ge(wo_full, b + 1)
                dve.wait_ge(xbo_ok, b + 1)
                dve.scalar_tensor_tensor(out=x1[:, :, :].rearrange("p t f -> p (t f)"), in0=misc[bank_of("wo")][:, 0:QT * E],
                                         scalar=tgates[:, 0:1], in1=x_bo[:, :, :].rearrange("p t f -> p (t f)"),
                                         op0=ALU.mult, op1=ALU.add).then_inc(x1_ok, 1)

            def logits_out(b):
                dve.wait_ge(lg_full, b + 1)
                dve.tensor_tensor(logits[:, bass.ds(b * QT, QT), :],
                                  misc[bank_of("logits")][:, 0:QT * NEXP].rearrange("p (t e) -> p t e", e=NEXP),
                                  rb_row.unsqueeze(1).to_broadcast([P, QT, NEXP]), ALU.add).then_inc(lg_ok, 1)

            count = [0]

            def router(half, meanwhile=lambda: None, midway=lambda: None):
                def step(ins):
                    count[0] += 1
                    ins.then_inc(rt_step, 1)
                    dve.wait_ge(rt_step, count[0])

                n_t = TT // 2
                tiles = slice(half * n_t, (half + 1) * n_t)

                def bc(a):
                    return a.unsqueeze(2).to_broadcast([P, n_t, NEXP])

                z, ez, pr, tmp = (rt[:, k, tiles, :] for k in range(4))
                flat = [a.rearrange("p t e -> p (t e)") for a in (z, ez, pr, tmp)]
                low, total, above = (rs[:, k, tiles] for k in range(3))
                dve.wait_ge(lg_ok, (half + 1) * B // 2)
                step(dve.tensor_reduce(low, logits[:, tiles, :], AX_X, ALU.max))
                dve.tensor_tensor(z, logits[:, tiles, :], bc(low), ALU.subtract).then_inc(z_ok, 1)
                meanwhile()
                dve.wait_ge(rexp_ok, half + 1)
                step(dve.tensor_reduce(total, ez, AX_X, ALU.add))
                step(dve.reciprocal(total, total))
                step(dve.tensor_tensor(pr, ez, bc(total), ALU.mult))
                for n in range(tiles.start, tiles.stop):
                    last = dve.max(top8[:, n, :], rt[:, 2, n, :])
                step(last)
                midway()
                fourth = bc(top8[:, tiles, TOPK - 1])
                step(dve.tensor_tensor(z, pr, fourth, ALU.is_gt))
                step(dve.tensor_reduce(above, z, AX_X, ALU.add))
                step(dve.tensor_tensor(ez, pr, fourth, ALU.is_equal))
                dve.wait_ge(ld_c, 64)
                step(dve.tensor_tensor_scan(flat[3], notfirst[:, 0:n_t * NEXP], flat[1], 0.0, ALU.mult, ALU.add))
                step(dve.tensor_tensor(tmp, tmp, bc(above), ALU.add))
                step(dve.scalar_tensor_tensor(out=flat[3], in0=flat[3], scalar=float(TOPK), in1=flat[1], op0=ALU.is_le, op1=ALU.mult))
                step(dve.tensor_tensor(z, z, tmp, ALU.add))
                step(dve.tensor_tensor(z, z, pr, ALU.mult))
                step(dve.tensor_reduce(total, z, AX_X, ALU.add))
                step(dve.reciprocal(total, total))
                dve.tensor_tensor(ez, z, bc(total), ALU.mult).then_inc(cw_ok, 1)

            def weights_out(half, out):
                for n in range(2):
                    c = 2 * half + n
                    dve.wait_ge(cwt_full, c + 1)
                    dve.tensor_copy(cw_t[:, c * CH:(c + 1) * CH], out[n][0:NEXP, :]).then_inc(cwt_ok, 1)

            def slots(b, p, before=None, after=None):
                for g in range(G):
                    last = g == G - 1 and not after
                    for j in range(8):
                        at_b, at_p, at_g, k, over = scores_at(b, p, g, j)
                        if not over or after:
                            row_max(at_b, at_p, at_g, k)
                            if k == 7:
                                minus_max(at_b, at_p, at_g)
                        if g == 3 and j == 4 and not after:
                            router(0)
                        if g == 3 and j == 5 and before:
                            logits_out(b - 1)
                        if j == 5 and not last:
                            if g < G - 1:
                                shift(b, p, g + 1, 1 - p if g == 2 and after else None)
                            else:
                                shift(b + 1, 1 - p, 0)
                        step = g * 8 + j
                        if after:
                            if step == 0:
                                ln_x(b + 1)
                            if step == 2:
                                k_lo_half(b + 1)
                            if step == 10:
                                q_lo_half(b + 1)
                        if before:
                            if step == 6:
                                normalise(b - 1, 1 - p, 0)
                            if step == 9:
                                normalise(b - 1, 1 - p, 1)
                            if step == 16:
                                residual(b - 1, 1 - p)
                        if 17 <= step <= 24:
                            steps = {17: [0], 18: [1, 2], 19: [3, 4], 20: [5, 6], 21: [7, 8], 22: [9, 10], 23: [11],
                                     24: [12]}[step]
                            if before:
                                ln_x1_statistics(b - 1, *steps)
                            else:
                                ln_x_statistics(slice(2 * QT, TT), 4 * QT + 11, *steps)
                        if before:
                            if step == 24:
                                ln_x1(b - 1)

            dve.memset(zero[:, :], 0.0).then_inc(zeroed_v, 1)
            dve.memset(v_one[:, 0, :, :, :], 0.0).then_inc(zeroed_v, 1)
            dve.wait_ge(zeroed_v, 2)
            dve.memset(v_one[:, 0, :, :, D:D + 1].rearrange("p t h r -> p (t h) r"), 1.0).then_inc(zeroed_v, 1)
            dve.wait_ge(ld_x0, 16)
            ln_x_statistics(slice(0, 2 * QT), 0, *range(13))
            ln_x(0)
            dve.wait_ge(ld_cols, 16)
            k_lo_half(0)
            dve.wait_ge(ld_sel, 16)
            dve.tensor_copy(sel[:, :, :, :].rearrange("p m g r -> p (m g r)"), selraw).then_inc(sel_ok, 1)
            dve.tensor_copy(attn[:, 0, :], cols[:, 3:4].to_broadcast([P, P])).then_inc(bvo_ok, 1)
            dve.memset(minus_masked[:, :], -MASKED).then_inc(zeroed_v, 1)
            dve.memset(ones[:, :], 1.0).then_inc(zeroed_v, 1)
            dve.memset(neg_m[:, :, :, :], 0.0).then_inc(zeroed_v, 1)
            dve.wait_ge(ld_ident, 16)
            dve.tensor_copy(ident_b[:, :], ident[:, :]).then_inc(ident_ok, 1)
            q_lo_half(0)
            dve.wait_ge(bvo_full, 1)
            dve.wait_ge(ld_rows, 16)
            dve.tensor_tensor(tg_bo[:, :], banks[:, 5, 0:E], rows[:, 0:E], ALU.add).then_inc(bvo_ok, 1)
            dve.wait_ge(bvo_ok, 2)
            dve.wait_ge(tanh_ok, 1)
            dve.tensor_scalar(tg_bo[:, :], tg_bo[:, :], tgates[:, 0:1], None, ALU.mult).then_inc(tgbo_ok, 1)
            for k in range(8):
                row_max(0, 0, 0, k)
            minus_max(0, 0, 0)
            row_max(0, 0, 1, 0)
            shift(0, 0, 0, 0)
            for k in range(1, EARLY - 8):
                row_max(0, 0, 1, k)
            dve.wait_ge(ld_x, 16)
            slots(0, 0, before=False, after=True)
            with dve.Fori(1, B - 2, 2) as i:
                slots(i, 1, before=True, after=True)
                slots(i + 1, 0, before=True, after=True)
            slots(B - 1, 1, before=True, after=False)

            def weigh(v, k, weights):
                dve.wait_ge(gelu_ok, v + 1)
                if not (isinstance(v, int) and v < 2):
                    dve.wait_ge(g_hi_ok, v - 1)
                    dve.wait_ge(g_lo_ok, v - 1)
                dve.tensor_tensor(gw[k % 2], gel[k % 2], weights, ALU.mult).then_inc(gw_ok, 1)

            def lo_half(v, par):
                dve.wait_ge(g_hi_ok, v + 1)
                dve.tensor_tensor(g_lo[par], gw[par], g_hi[par].bitcast(F32), ALU.subtract).then_inc(g_lo_ok, 1)

            def first_weigh(v):
                e, k = FIRST[v]
                dve.wait_ge(ld_first[e], 16 + 16 * (k // 2))
                weigh(v, k, cw_first[e])

            def expert(e, p):
                for k in range(UNITS_E):
                    if k == 0:
                        dve.wait_ge(ld_cw[p], e * 8 - (16 if p == 0 else 24))
                    weigh(e * UNITS_E + k, k, cw[p][:, (k // 2) * HALF:(k // 2 + 1) * HALF])
                    lo_half(e * UNITS_E + (k - 1), (k - 1) % 2)

            normalise(B - 1, 1, 0)
            normalise(B - 1, 1, 1)
            weights_out(0, [banks[:, 2, :], banks[:, 3, :]])
            residual(B - 1, 1)
            ln_x1_statistics(B - 1, *range(13))
            ln_x1(B - 1)
            first_weigh(0)
            first_weigh(1)
            logits_out(B - 1)
            router(1, lambda: (lo_half(0, 0), first_weigh(2)), lambda: first_weigh(3))
            first_weigh(POOLS)
            weights_out(1, acc[2:4])
            dve.wait_ge(g_lo_ok, POOLS)
            lo_half(POOLS, POOLS % 2)
            first_weigh(POOLS + 1)
            for v in range(POOLS + 2, len(FIRST)):
                first_weigh(v)
                lo_half(v - 1, (v - 1) % 2)
            with dve.Fori(EARLY_E, NEXP - 1, 2) as i:
                expert(i, 0)
                expert(i + 1, 1)
            lo_half(NEXP * UNITS_E - 1, 1)
            for c in range(4):
                if c % 2 == 0:
                    dve.wait_ge(ff_done, NEXP * UNITS_E - (2 - c))
                cols_c = x1_t[:, c * CH:(c + 1) * CH]
                dve.scalar_tensor_tensor(out=cols_c, in0=acc[c], scalar=tgates[:, 1:2], in1=cols_c, op0=ALU.mult,
                                         op1=ALU.add).then_inc(out_ok, 1)

        @block.tensor
        def _(pe):
            def taken(task, b):
                if task.startswith("max_t"):
                    return qshift_ok, b * 4 + (int(task[-1]) + 1)
                if task.startswith("heads_t"):
                    return attn_ok, b * 2 + (int(task[-1]) + 1)
                if task.startswith("q_stack"):
                    return qs_ok, b * 2 + (int(task[-1]) + 1)
                if task.startswith("k_stack"):
                    return ks_ok, b * 4 + (int(task[-1]) + 1)
                return {"xn_t": xnt_ok, "attn_t": attnt_ok, "q": qlo_ok, "k": klo_ok, "v": v_ok, "wo": x1_ok,
                        "x1_t": x1t_ok, "logits": lg_ok}[task], b + 1

            def misc_bank(task, b):
                if task == "v" and not isinstance(b, int):
                    return misc[bank_of(task)]
                for n in range(MISC_AT[task] - 1, -2 * len(MISC), -1):
                    before, other, bank = MISC[n % len(MISC)]
                    at = b + (n // len(MISC) + other)
                    if bank == bank_of(task) and (not isinstance(at, int) or 0 <= at < B):
                        pe.wait_ge(*taken(before, at))
                        break
                return misc[bank_of(task)]

            def transpose_xn(b):
                bank = misc_bank("xn_t", b)
                pe.wait_ge(ln_done[0], b * 2 + 4)
                for q in range(QT):
                    last = pe.transpose(bank[:, q * P:(q + 1) * P], xn[:, q, :], ident[:, :])
                last.then_inc(xnt_full, 1)

            def project_q(b):
                bank = misc_bank("q", b)
                pe.wait_ge(xnt_ok, b + 2)
                pe.matmul(bank[:, 0:NQ], wqkvo[:, 0, :], xn_t[:, :], start=True, stop=True).then_inc(q_full, 1)

            def project_k(b, p):
                bank = misc_bank("k", b)
                pe.wait_ge(ld_ctx[p], ctx_count(b + 1, p))
                pe.matmul(bank, wqkvo[:, 1, :], ctx_t[:, p, :], start=True, stop=True).then_inc(k_full, 1)

            def project_v(b, p):
                bank = misc_bank("v", b)
                for kt in range(KT):
                    last = pe.matmul(bank[:, kt * E:(kt + 1) * E], ctx_t[:, p, kt * P:(kt + 1) * P], wqkvo[:, 2, :],
                                     start=True, stop=True)
                last.then_inc(v_full, 1)

            def stack_q(b, n):
                bank = misc_bank(f"q_stack{n}", b)
                pe.wait_ge(qlo_ok, b + 2)
                for s in range(2):
                    out, g = bank[:, s * NQ:(s + 1) * NQ], 2 * n + s
                    pe.matmul(out, sel[:, 0, g, :], q_hi[:, :], start=True, stop=False)
                    last = pe.matmul(out, sel[:, 1, g, :], q_lo[:, :], start=False, stop=True)
                last.then_inc(qs_full, 1)

            def stack_k(b, g):
                bank = misc_bank(f"k_stack{g}", b)
                pe.wait_ge(klo_ok, b + 2)
                pe.matmul(bank, sel[:, 2, g, :], k_hi[:, :], start=True, stop=False)
                pe.matmul(bank, sel[:, 3, g, :], k_lo[:, :], start=False, stop=True).then_inc(ks_full, 1)

            def transpose_heads(b, q):
                bank = misc_bank(f"heads_t{q}", b)
                pe.wait_ge(heads_out, b * 4)
                for g in range(G):
                    last = pe.transpose(bank[:, g * P:(g + 1) * P], out_g[:, g, q * P:(q + 1) * P], ident[:, :])
                last.then_inc(ht_full, 1)

            def transpose_attn(b):
                bank = misc_bank("attn_t", b)
                pe.wait_ge(attn_ok, b * 2)
                for q in range(QT):
                    last = pe.transpose(bank[:, q * P:(q + 1) * P], attn[:, q, :], ident[:, :])
                last.then_inc(at_full, 1)

            def project_o(b):
                bank = misc_bank("wo", b)
                pe.wait_ge(attnt_ok, b)
                for q in range(QT):
                    last = pe.matmul(bank[:, q * E:(q + 1) * E], attn_t[:, q * P:(q + 1) * P], wqkvo[:, 3, :],
                                     start=True, stop=True)
                last.then_inc(wo_full, 1)

            def transpose_x1(b):
                bank = misc_bank("x1_t", b)
                pe.wait_ge(ln_done[1], b * 2)
                for q in range(QT):
                    pe.transpose(bank[:, q * P:(q + 1) * P], xn2[:, q, :], ident[:, :])
                for q in range(QT):
                    last = pe.transpose(bank[:, NQ + q * P:NQ + (q + 1) * P], x1[:, q, :], ident[:, :])
                last.then_inc(x1t_full, 1)

            def route(b):
                bank = misc_bank("logits", b)
                pe.wait_ge(xn2t_ok, b)
                for q in range(QT):
                    last = pe.matmul(bank[:, q * NEXP:(q + 1) * NEXP], xn2_t[:, q * P:(q + 1) * P], rw[:, :],
                                     start=True, stop=True)
                last.then_inc(lg_full, 1)

            def transpose_weights(half, out):
                pe.wait_ge(cw_ok, half + 1)
                if half:
                    pe.wait_ge(lg_ok, B)
                    pe.wait_ge(x1t_ok, B)
                for c in range(2):
                    for n in range(4):
                        last = pe.transpose(out[c][0:NEXP, n * P:(n + 1) * P], rt[:, 1, 8 * half + 4 * c + n, :], ident[:, :])
                    last.then_inc(cwt_full, 1)

            def transpose_max(b, g, flag=None):
                bank = misc_bank(f"max_t{(g + 1) % G}", b)
                pe.wait_ge(negm_ok, b * 4 + (g + 2))
                for q in range(QT):
                    last = pe.transpose(bank[:, q * P:(q + 1) * P], neg_m[:, (g + 1) % 2, q, :], ident[:, :])
                if flag is not None:
                    pe.wait_ge(maskt_ok, b + 2)
                    last = pe.matmul(bank[0:1, NQ:NQ + 1], mask_sum[:, flag:flag + 1], ones[:, :], start=True, stop=True)
                last.then_inc(mt_full, 1)

            def scores(b, p, g, k):
                qt, i = k // HG, k % HG
                if k == 0:
                    pe.wait_ge(pad_ok, b * 4 + (g + 1))
                    if g % 2 == 0:
                        pe.wait_ge(qs_ok, b * 2 + (g // 2 + 1))
                before = {0: -1, 1: 0, 2: -2}.get(k, k - SC + 1)
                wait(pe, max_done, b * 32 + (g * 8 + before))
                pe.matmul(sc[k % SC], q_stack[:, p, g, qt * P:(qt + 1) * P], k_pad[:, p, HG * g + i, :],
                          start=True, stop=True).then_inc(sc_full, 1)

            def scores_t(b, p, g, j, masked):
                kt, pair = j // 2, j % 2
                if j == 0:
                    pe.wait_ge(qshift_ok, b * 4 + (g + 1))
                    if g == 0:
                        pe.wait_ge(maskt_ok, b + 1)
                wait(pe, exp_done, b * 32 + (g * 8 + j - 1))
                if masked:
                    pe.matmul(st[j % 2], ident_b[:, :], maskt[:, p, kt, :].unsqueeze(1).to_broadcast([P, 2, NQ]),
                              start=True, stop=False)
                for s in range(2):
                    last = pe.matmul(st[j % 2][:, s * NQ:(s + 1) * NQ],
                                     k_pad[:, p, HG * g + 2 * pair + s, kt * P:(kt + 1) * P], q_shift[:, g % 2, :],
                                     start=not masked, stop=not masked or s == 1)
                last.then_inc(st_full, 1)

            def values(b, p, g, kt):
                if kt == 0:
                    if g == 0:
                        pe.wait_ge(v_ok, b + 1)
                    if isinstance(b, int) and b == 0 and g == 0:
                        pe.wait_ge(tgbo_ok, 1)
                    else:
                        pe.wait_ge(heads_out, b * 4 + g)
                pe.wait_ge(exp_done, b * 32 + (g * 8 + 2 * kt + 2))
                for i in range(HG):
                    last = pe.matmul(ov[R * i:R * (i + 1), :], v_one[:, p, kt, HG * g + i, :],
                                     probs[:, kt, i * NQ:(i + 1) * NQ], start=kt == 0, stop=kt == KT - 1)
                last.then_inc(pv_done, 1)

            def slots(b, p, before=None, after=None):
                wait_apart(pe, flag_ok, b + 1)
                kept = pe.value_load(all_kept[0:1, p:p + 1])
                with pe.If(kept > 0):
                    batch(b, p, before, after, masked=False)
                with pe.If(kept < 1):
                    batch(b, p, before, after, masked=True)

            def batch(b, p, before, after, masked):
                for g in range(G):
                    last = g == G - 1 and not after
                    for j in range(8):
                        if j == 5 and not last:
                            transpose_max(b, g, 1 - p if g == 2 and after else None)
                        scores_t(b, p, g, j, masked)
                        at_b, at_p, at_g, k, over = scores_at(b, p, g, j)
                        if not over or after:
                            scores(at_b, at_p, at_g, k)
                        if j == 1 and g:
                            values(b, p, g - 1, KT - 1)
                        if j == 1 and not g and before:
                            values(b - 1, 1 - p, G - 1, KT - 1)
                        if j in (3, 5, 7):
                            values(b, p, g, (j - 3) // 2)
                        step = g * 8 + j
                        if after:
                            if step == 0:
                                project_k(b, 1 - p)
                            if step == 1:
                                project_v(b, 1 - p)
                            if step == 3:
                                transpose_xn(b)
                            if step == 8:
                                project_q(b)
                        if before:
                            if step in (5, 8):
                                transpose_heads(b, (5, 8).index(step))
                            if step == 11:
                                transpose_attn(b)
                        if step == 13 and after:
                            stack_k(b, 0)
                        if step == 15 and before:
                            project_o(b)
                        if after:
                            if step in (16, 24):
                                stack_q(b, (16, 24).index(step))
                            if step in (18, 19):
                                stack_k(b, step - 17)
                            if step == 22:
                                stack_k(b, 3)
                        if before:
                            if step == 26:
                                transpose_x1(b)
                            if step == 28:
                                route(b)

            pe.wait_ge(ld_w, 16)
            project_k(-1, 0)
            project_v(-1, 0)
            pe.wait_ge(ld_ident, 16)
            transpose_xn(-1)
            project_q(-1)
            pe.wait_ge(sel_ok, 1)
            stack_k(-1, 0)
            stack_q(-1, 0)
            pe.wait_ge(bvo_ok, 1)
            pe.matmul(banks[:, 5, 0:E], attn[:, 0, :], wqkvo[:, 3, :], start=True, stop=True).then_inc(bvo_full, 1)
            stack_k(-1, 1)
            for k in range(3):
                scores(0, 0, 0, k)
            stack_k(-1, 2)
            for k in range(3, 8):
                scores(0, 0, 0, k)
            stack_k(-1, 3)
            scores(0, 0, 1, 0)
            stack_q(-1, 1)
            pe.wait_ge(zeroed_v, 6)
            transpose_max(-1, 3, 0)
            for k in range(1, EARLY - 8):
                scores(0, 0, 1, k)
            pe.wait_ge(ident_ok, 1)
            pe.wait_ge(zeroed_v1, 2)
            slots(0, 0, before=False, after=True)
            pe.wait_ge(ld_c, 64)
            with pe.Fori(1, B - 2, 2) as i:
                slots(i, 1, before=True, after=True)
                slots(i + 1, 0, before=True, after=True)
            slots(B - 1, 1, before=True, after=False)

            def hidden(v, k, e, p, split=None):
                mt, half = k % 2, k // 2
                w_hi, w_lo = halves_of(e, p)
                if split is not None:
                    pe.wait_ge(w_lo_ok, split)
                wait(pe, gelu_ok, v - 1)
                w = slice(mt * P, (mt + 1) * P)
                for c in range(2):
                    h = slice(half * HALF + c * CH, half * HALF + (c + 1) * CH)
                    pe.matmul(hid[k % 2][:, c, :], w_hi[:, w], h_lo[:, h], start=True, stop=False)
                    pe.matmul(hid[k % 2][:, c, :], w_lo[:, w], h_hi[:, h], start=False, stop=False)
                    last = pe.matmul(hid[k % 2][:, c, :], w_hi[:, w], h_hi[:, h], start=False, stop=True)
                last.then_inc(hid_full, 1)

            def output(v, k, e, p):
                mt, half = k % 2, k // 2
                w_hi, w_lo = halves_of(e, p)
                pe.wait_ge(g_lo_ok, v + 1)
                w = slice(FF + mt * E, FF + (mt + 1) * E)
                for c in range(2):
                    g, out = slice(c * CH, (c + 1) * CH), acc[2 * half + c]
                    for wt, gt in ((w_hi, g_lo), (w_lo, g_hi), (w_hi, g_hi)):
                        last = pe.matmul(out, wt[:, w], gt[k % 2][:, g], start=False, stop=True, skip_group_check=True)
                last.then_inc(ff_done, 1)

            def sum_b2(half):
                for c in (2 * half, 2 * half + 1):
                    pe.wait_ge(cwt_ok, c + 1)
                    pe.matmul(acc[c], b2[:, :], cw_t[:, c * CH:(c + 1) * CH], start=True, stop=True)

            def first_hidden(v):
                if v < len(FIRST):
                    hidden(v, FIRST[v][1], FIRST[v][0], FIRST[v][0] % 2, FIRST[v][0] + 1)
                else:
                    hidden(v, v - len(FIRST), EARLY_E, 0, EARLY_E + 1)

            def first_output(v):
                output(v, FIRST[v][1], FIRST[v][0], FIRST[v][0] % 2)

            def expert(e, p, final=False):
                for k in range(UNITS_E):
                    v = e * UNITS_E + k
                    if k + AHEAD < UNITS_E:
                        hidden(v + AHEAD, k + AHEAD, e, p)
                    elif not final:
                        k_then = k + AHEAD - UNITS_E
                        hidden(v + AHEAD, k_then, e + 1, 1 - p, e + 2 if k_then == 0 else None)
                    output(v, k, e, p)

            values(B - 1, 1, G - 1, KT - 1)
            transpose_heads(B, 0)
            pe.wait_ge(hlo_ok, B // 2)
            first_hidden(0)
            transpose_heads(B, 1)
            transpose_weights(0, [banks[:, 2, :], banks[:, 3, :]])
            transpose_attn(B)
            project_o(B)
            pe.wait_ge(cwt_ok, 2)
            first_hidden(1)
            pe.wait_ge(heads_out, B * G)
            sum_b2(0)
            first_hidden(2)
            transpose_x1(B)
            route(B)
            first_hidden(3)
            first_output(0)
            for v in (1, 2):
                first_hidden(v + AHEAD)
                first_output(v)
            first_hidden(6)
            transpose_weights(1, acc[2:4])
            first_output(3)
            first_hidden(7)
            first_output(4)
            sum_b2(1)
            pe.wait_ge(hlo_ok, B)
            for v in range(5, len(FIRST)):
                first_hidden(v + AHEAD)
                first_output(v)
            with pe.Fori(EARLY_E, NEXP - 3, 2) as i:
                expert(i, 0)
                expert(i + 1, 1)
            expert(NEXP - 2, 0)
            expert(NEXP - 1, 1, final=True)


def kernel(x, ctx_1024, mask_BxSxS2_bf1, g_xattn, g_ffn, L0_xattn_Wq, L0_xattn_bq, L0_xattn_Wk, L0_xattn_bk,
           L0_xattn_Wv, L0_xattn_bv, L0_xattn_Wo, L0_xattn_bo, L0_ffn_router_w, L0_ffn_router_b, L0_ffn_w1,
           L0_ffn_b1, L0_ffn_w2, L0_ffn_b2):
    import concourse.bacc as bacc
    from concourse.bass_utils import run_bass_kernel_spmd

    def arr(a):
        return np.asarray(a)

    mask = arr(mask_BxSxS2_bf1).view(np.uint8)
    sel, ones = stack_selectors()
    notfirst = np.ones((TT, NEXP), np.float32)
    notfirst[:, 0] = 0.0
    w1 = arr(L0_ffn_w1)
    w2 = arr(L0_ffn_w2).reshape(NEXP, MT, P, E).transpose(0, 2, 1, 3).reshape(NEXP, P, MT * E)
    b1 = arr(L0_ffn_b1).reshape(NEXP, MT, P).transpose(2, 0, 1)
    arrays = {
        "x": arr(x).reshape(TOK, E),
        "ctx_t": arr(ctx_1024).transpose(0, 2, 1),
        "maskq": mask,
        "maskt": mask.transpose(0, 2, 1),
        "wqkvo": np.concatenate([arr(w).T for w in (L0_xattn_Wq, L0_xattn_Wk, L0_xattn_Wv, L0_xattn_Wo)], axis=1),
        "cols": np.stack([arr(L0_xattn_bq), arr(L0_xattn_bk), ones[:, 0], arr(L0_xattn_bv)], axis=1),
        "rows": np.concatenate([arr(a).reshape(1, -1) for a in (L0_xattn_bo, L0_ffn_router_b, g_xattn,
                                                                 g_ffn)], axis=1),
        "ident": np.eye(P, dtype=np.float32),
        "sel": sel,
        "notfirst": notfirst.reshape(1, -1),
        "router_w": arr(L0_ffn_router_w),
        "b2": arr(L0_ffn_b2),
        "b1": b1,
        "experts": np.concatenate([w1, w2], axis=2),
    }
    arrays = {k: np.ascontiguousarray(a) for k, a in arrays.items()}
    nc = bacc.Bacc("TRN2", target_bir_lowering=False, num_devices=1)
    tensors = {k: nc.dram_tensor("in_" + k, a.shape, mybir.dt.from_np(a.dtype), kind="ExternalInput").ap()
               for k, a in arrays.items()}
    tensors["cw"] = nc.dram_tensor("expert_weights", (NEXP, TOK), F32, kind="Internal").ap()
    tensors["out"] = nc.dram_tensor("out", (E, TOK), F32, kind="ExternalOutput").ap()
    build(nc, tensors)
    r = run_bass_kernel_spmd(nc, [{"in_" + k: a for k, a in arrays.items()}], core_ids=[0])
    return np.ascontiguousarray(r.results[0]["out"].T).reshape(B, NQ, E)
```
